# Optimizing a Trainium2 kernel written in Bass

```python
import numpy as np
import jax
import jax.numpy as jnp

def _softmax(x, axis=-1):
    return jax.nn.softmax(x, axis=axis)
def _gelu(x):
    return jax.nn.gelu(x, approximate=True)
def _silu(x):
    return jax.nn.silu(x)
def _sigmoid(x):
    return jax.nn.sigmoid(x)
def _layernorm(x, axis=-1, eps=1e-5):
    m = jnp.mean(x, axis=axis, keepdims=True)
    v = jnp.var(x, axis=axis, keepdims=True)
    return (x - m) / jnp.sqrt(v + eps)
def _scatter_add(tgt, idx, src, axis=0):
    return tgt.at[idx].add(src)
def _segment_sum(src, seg, n):
    return jax.ops.segment_sum(src, seg, n)

kernel_name = 'mk_metaformer_d1_conv_nchw256_42d1e8'

def setup_inputs(seed: int = 0):
    np.random.seed(seed)
    _w = jnp.asarray
    def _rec_inputs():
        import jax
        import jax.numpy as jnp
        _gk = jax.random.key(seed)
        x = -0.0002928 + 1 * jax.random.normal(jax.random.fold_in(_gk, 1), (4, 256, 64, 64), jnp.float32)
        return x
    x = _rec_inputs()
    def _L0_conv_setup():
        import jax, jax.numpy as jnp
        import numpy as np
        B, C, H, W = (4, 256, 64, 64)
        D = 64
        key = jax.random.key(seed)
        ks = jax.random.split(key, 7)
        s_in = 1.0 / np.sqrt(C)
        return {'x': jax.random.normal(ks[0], (B, C, H, W), dtype=jnp.float32), 'wq': jax.random.uniform(ks[1], (D, C), jnp.float32, -s_in, s_in), 'bq': jax.random.uniform(ks[2], (D,), jnp.float32, -s_in, s_in), 'wk': jax.random.uniform(ks[3], (D, C), jnp.float32, -s_in, s_in), 'bk': jax.random.uniform(ks[4], (D,), jnp.float32, -s_in, s_in), 'wv': jax.random.uniform(ks[5], (C, C), jnp.float32, -s_in, s_in), 'bv': jax.random.uniform(ks[6], (C,), jnp.float32, -s_in, s_in)}
    _L0_conv_all = _L0_conv_setup()
    _L0_conv_in = {k: v for k, v in _L0_conv_all.items() if k in ('wq', 'bq', 'wk', 'bk', 'wv', 'bv', )}
    del _L0_conv_all

    def _L0_ffn_setup():
        import jax, jax.numpy as jnp
        import numpy as np
        B, S, D = (8, 4096, 256)
        H = 4 * D
        CAPACITY = 0.5
        key = jax.random.key(seed)
        ks = jax.random.split(key, 6)
        x = jax.random.normal(ks[0], (B, S, D), dtype=jnp.float32)
        attention_mask = jnp.zeros((B, 1, 1, S), dtype=jnp.float32)
        wr = jax.random.normal(ks[1], (D, 1), dtype=jnp.float32) * 0.02
        br = jnp.zeros((1,), dtype=jnp.float32)
        w1 = jax.random.normal(ks[2], (D, H), dtype=jnp.float32) * 0.02
        b1 = jnp.zeros((H,), dtype=jnp.float32)
        w2 = jax.random.normal(ks[3], (H, D), dtype=jnp.float32) * 0.02
        b2 = jnp.zeros((D,), dtype=jnp.float32)
        return {'x': x, 'attention_mask': attention_mask, 'wr': wr, 'br': br, 'w1': w1, 'b1': b1, 'w2': w2, 'b2': b2}
    _L0_ffn_all = _L0_ffn_setup()
    _L0_ffn_in = {k: v for k, v in _L0_ffn_all.items() if k in ('attention_mask', 'wr', 'br', 'w1', 'b1', 'w2', 'b2', )}
    del _L0_ffn_all

    return {
        "x": x,
        "L0_conv_wq": _L0_conv_in["wq"],
        "L0_conv_bq": _L0_conv_in["bq"],
        "L0_conv_wk": _L0_conv_in["wk"],
        "L0_conv_bk": _L0_conv_in["bk"],
        "L0_conv_wv": _L0_conv_in["wv"],
        "L0_conv_bv": _L0_conv_in["bv"],
        "L0_ffn_attention_mask": _L0_ffn_in["attention_mask"],
        "L0_ffn_wr": _L0_ffn_in["wr"],
        "L0_ffn_br": _L0_ffn_in["br"],
        "L0_ffn_w1": _L0_ffn_in["w1"],
        "L0_ffn_b1": _L0_ffn_in["b1"],
        "L0_ffn_w2": _L0_ffn_in["w2"],
        "L0_ffn_b2": _L0_ffn_in["b2"],
    }

def reference(x, L0_conv_wq, L0_conv_bq, L0_conv_wk, L0_conv_bk, L0_conv_wv, L0_conv_bv, L0_ffn_attention_mask, L0_ffn_wr, L0_ffn_br, L0_ffn_w1, L0_ffn_b1, L0_ffn_w2, L0_ffn_b2):
    import jax
    import jax.numpy as jnp
    def _L0_conv_ref(x, wq, bq, wk, bk, wv, bv):
        import jax, jax.numpy as jnp
        import numpy as np
        B, C, H, W = (4, 256, 64, 64)
        D = 64
        b, c, h, w = x.shape
        xf = x.reshape(b, c, h * w)
        q = jnp.einsum('dc,bcn->bnd', wq, xf) + bq
        k = jnp.einsum('dc,bcn->bdn', wk, xf) + bk[:, None]
        v = jnp.einsum('oc,bcn->bon', wv, xf) + bv[:, None]
        attn = jax.nn.softmax(jnp.einsum('bnd,bdm->bnm', q, k), axis=-1)
        out = jnp.einsum('bcm,bnm->bcn', v, attn)
        return out.reshape(b, c, h, w)

    def _L0_ffn_ref(x, attention_mask, wr, br, w1, b1, w2, b2):
        import jax, jax.numpy as jnp
        import numpy as np
        B, S, D = (8, 4096, 256)
        H = 4 * D
        CAPACITY = 0.5
        b, s, d = x.shape
        weights = (jnp.einsum('bsd,do->bso', x, wr) + br)[..., 0]
        k = max(1, int(CAPACITY * s))
        kk = k - 1 if k > 1 else 1
        _, idx = jax.lax.top_k(weights, k)
        sel_idx = idx[:, :kk]
        sel = jnp.take_along_axis(x, sel_idx[:, :, None], axis=1)
        h = jax.nn.gelu(jnp.einsum('bkd,dh->bkh', sel, w1) + b1)
        y = jnp.einsum('bkh,hd->bkd', h, w2) + b2
        w_sel = jnp.take_along_axis(weights, sel_idx, axis=1)
        y = y * w_sel[..., None]
        batch_idx = jnp.arange(b)[:, None]
        processed = jnp.zeros_like(x).at[batch_idx, sel_idx].set(y)
        return processed + x

    def _gn(v, G=32, eps=1e-5):
        B_, C_, H_, W_ = v.shape
        g = v.reshape(B_, G, C_ // G, H_, W_)
        m = jnp.mean(g, axis=(2, 3, 4), keepdims=True)
        s = jnp.var(g, axis=(2, 3, 4), keepdims=True)
        return ((g - m) / jnp.sqrt(s + eps)).reshape(v.shape)

    def _ln_c(v, eps=1e-6):
        m = jnp.mean(v, axis=1, keepdims=True)
        s = jnp.var(v, axis=1, keepdims=True)
        return (v - m) / jnp.sqrt(s + eps)

    def _ln_t(v, eps=1e-5):
        m = jnp.mean(v, axis=-1, keepdims=True)
        s = jnp.var(v, axis=-1, keepdims=True)
        return (v - m) / jnp.sqrt(s + eps)

    def _to_tokens(v):
        B_, C_, H_, W_ = v.shape
        return v.reshape(B_, C_, H_ * W_).transpose(0, 2, 1)
    def _from_tokens(t, like):
        B_, C_, H_, W_ = like.shape
        return t.transpose(0, 2, 1).reshape(B_, C_, H_, W_)

    x = x + _L0_conv_ref(_ln_c(x), L0_conv_wq, L0_conv_bq, L0_conv_wk, L0_conv_bk, L0_conv_wv, L0_conv_bv)
    t = _to_tokens(x)
    t = t + _L0_ffn_ref(_ln_t(t), L0_ffn_attention_mask, L0_ffn_wr, L0_ffn_br, L0_ffn_w1, L0_ffn_b1, L0_ffn_w2, L0_ffn_b2)
    x = _from_tokens(t, x)
    return x


_drawn_inputs = setup_inputs


def setup_inputs(seed=0):
    import zlib

    import numpy as np

    out = dict(_drawn_inputs(seed))
    spreads = {'L0_ffn_b1': (0.0, 0.8), 'L0_ffn_b2': (0.0, 0.709)}
    factors = {'L0_conv_bq': 3.522,
     'L0_conv_bk': 8.0,
     'L0_ffn_wr': 3.76,
     'L0_ffn_w1': 4.452,
     'L0_ffn_w2': 4.149}
    for name, (base, spread) in spreads.items():
        noise = np.random.default_rng([zlib.crc32(name.encode()), seed]).standard_normal(out[name].shape)
        drawn = base * np.exp(spread * noise) if base else spread * noise
        out[name] = jnp.asarray(drawn.astype(out[name].dtype))
    for name, factor in factors.items():
        out[name] = (out[name] * factor).astype(out[name].dtype)
    return out
```

```python
from contextlib import ExitStack

import concourse.bass as bass
from concourse import mybir

F32 = mybir.dt.float32
F16 = mybir.dt.float16
I32 = mybir.dt.int32
U32 = mybir.dt.uint32
ALU = mybir.AluOpType
ACT = mybir.ActivationFunctionType
AX = mybir.AxisListType

P = 128
B = 4
N = 4096
C = 256
D = 64
HID = 1024
CC = C // P
HC = HID // P
NT = N // P
KEEP = N // 2
GRP = 4
NG = NT // GRP
GW = GRP * P
QB = 256
QT = QB // P
NB = N // QB
STEPS = NT // 2
UNITS = QT * (N // 512)
VW = 514
VLO = 258
PAY = 258
ROWS = B * KEEP
FB = 256
FT = FB // P
NF = ROWS // FB
RING = 4
NI = NF // RING
SHIFT = 6.0
UNIT_OF = [2, 2, 2, 2, 1, 1, 1, 1, 1, 1, 1, 1, 0, 0, 0, 0]
assert sum(UNIT_OF) == UNITS and len(UNIT_OF) == STEPS
BIG = 100000.0


def build(nc, x, wq, wk, wv, bq, bk, bv, wr, br, w1, b1, w2, b2, out):
    ctx = ExitStack()
    with ctx:
        def sb(name, shape, dt):
            return ctx.enter_context(nc.sbuf_tensor(name, shape, dt))

        def sem(name):
            return ctx.enter_context(nc.semaphore(name))

        packed = nc.dram_tensor("packed_rows", (ROWS, PAY), F32, kind="Internal").ap()
        x_v = x.rearrange("(g t p) c -> g p t c", p=P, t=GRP)
        out_v = out.rearrange("(k t p) c -> k p t c", p=P, t=QT)
        packed_v = packed.rearrange("(f t p) c -> f p t c", p=P, t=FT)

        ident = sb("ident", [P, P], F16)
        ones16 = sb("ones16", [P, P], F16)
        tri16 = sb("tri16", [P, P], F16)
        wq_s = sb("wq_s", [P, 2, CC, P], F16)
        wk_s = sb("wk_s", [P, 2, CC, P], F16)
        wv_s = sb("wv_s", [P, 2, CC, C], F16)
        w1_s = sb("w1_s", [P, 2, CC, HID], F16)
        w2_s = sb("w2_s", [P, 2, HC, C], F16)
        bq_s = sb("bq_s", [P, 1], F32)
        bk_s = sb("bk_s", [P, 1], F32)
        br_s = sb("br_s", [P, 1], F32)
        b1_s = sb("b1_s", [P, HC], F32)
        bv_s = sb("bv_s", [P, 2, C], F32)
        wr_s = sb("wr_s", [P, C], F32)
        b2_s = sb("b2_s", [P, FT, C], F32)
        xs = sb("xs", [P, NT, C], F32)
        ka = sb("ka", [P, N], F16)
        kb = sb("kb", [P, N], F16)
        qa = sb("qa", [P, N], F16)
        qb = sb("qb", [P, N], F16)
        vs = sb("vs", [P, NT, VW], F16)
        pay = sb("pay", [P, NT, PAY], F32)
        y32 = sb("y32", [P, GRP, C], F32)
        yhl = sb("yhl", [P, 2, GRP, C], F16)
        yt = sb("yt", [P, 2, CC, GW], F16)
        v32 = sb("v32", [P, 2, 2, C], F32)
        st = sb("st", [P, GRP, 6], F32)
        mv = sb("mv", [P, GRP, 2], F32)
        ve = sb("ve", [P, GRP], F32)
        rstd = sb("rstd", [P, GRP], F32)
        mhalf = sb("mhalf", [P, GRP], F32)
        p32 = sb("p32", [P, 2, 2, QB], F32)
        phi = sb("phi", [P, 4, 2, QB], F16)
        plo = sb("plo", [P, 4, 2, QB], F16)
        mpart = sb("mpart", [P, QT, 8], F32)
        mrow = sb("mrow", [P, QT], F32)
        negm = sb("negm", [P, QT], F16)
        oe = sb("oe", [P, QT, C + 1], F32)
        rz = sb("rz", [P, QT], F32)
        tb = sb("tb", [P, QT, C], F32)
        est = sb("est", [P, QT, 6], F32)
        emv = sb("emv", [P, QT, 2], F32)
        eve = sb("eve", [P, QT], F32)
        erstd = sb("erstd", [P, QT], F32)
        wdot = sb("wdot", [P, QT], F32)
        wjunk = sb("wjunk", [P, QT, C], F32)
        lnb = sb("lnb", [P, QT, C], F32)
        res = sb("res", [P, QT, C], F32)
        wcol = sb("wcol", [P, NT], F32)
        tok = sb("tok", [P, NT], I32)
        tokf = sb("tokf", [P, NT], F32)
        rbase = sb("rbase", [P, 1], F32)
        cand_i = sb("cand_i", [P, 15], I32)
        cand1 = sb("cand1", [P, 15], F32)
        keym = sb("keym", [P, NT], I32)
        key = sb("key", [P, NT], I32)
        kpart = sb("kpart", [P, NT], I32)
        khi = sb("khi", [P, NT], F32)
        klo = sb("klo", [P, NT], F32)
        val = sb("val", [P, NT], F32)
        vtmp = sb("vtmp", [P, NT], F32)
        base = sb("base", [P, 2], F32)
        cand = sb("cand", [P, 15], F32)
        cmp = sb("cmp", [P, 15, NT], F32)
        cnt = sb("cnt", [P, 15], F16)
        isge = sb("isge", [P, 15], F32)
        nge = sb("nge", [P, 1], F32)
        gt16 = sb("gt16", [P, NT], F16)
        eq16 = sb("eq16", [P, NT], F16)
        sel16 = sb("sel16", [P, NT], F16)
        csum = sb("csum", [P, NT], F32)
        cexc = sb("cexc", [P, NT], F32)
        zeros = sb("zeros", [P, NT], F32)
        rank = sb("rank", [P, NT], F32)
        need = sb("need", [P, 1], F32)
        ngt = sb("ngt", [P, 1], F32)
        take = sb("take", [P, NT], F32)
        drop = sb("drop", [P, NT], F32)
        rowf = sb("rowf", [P, NT], F32)
        rowi = sb("rowi", [P, NT], I32)
        xs_flat = xs[:, :, :].rearrange("p a b -> p (a b)")
        used = [0]

        def in_xs(shape, dt):
            words = 1
            for n in shape:
                words *= n
            words = words // (2 if dt == F16 else 1)
            flat = xs_flat[:, used[0]:used[0] + words]
            used[0] += words
            assert used[0] <= NT * C
            names = "abcd"[:len(shape)]
            return (flat.bitcast(dt) if dt == F16 else flat).rearrange(
                f"p ({' '.join(names)}) -> p {' '.join(names)}", **dict(zip(names[1:], shape[1:])))

        rowb = in_xs([RING, FT, PAY], F32)
        thl = in_xs([2, FT, C], F16)
        tt = in_xs([2, 2, CC, FB], F16)
        h32 = in_xs([2, 2, FB], F32)
        hhi = in_xs([2, 2, FB], F16)
        hlo = in_xs([2, 2, FB], F16)
        zb = in_xs([RING, FT, C], F32)
        yb = tb

        stage = pay[:, :, :].rearrange("p a b -> p (a b)")
        sizes = [CC * P, CC * P, CC * C, CC * HID, HC * C]
        starts = [sum(sizes[:i]) for i in range(len(sizes))]
        staged = [stage[:, a:a + n] for a, n in zip(starts, sizes)]
        split = [w[:, :, :, :].rearrange("p h a b -> p h (a b)") for w in (wq_s, wk_s, wv_s, w1_s, w2_s)]

        bank = [ctx.enter_context(nc.psum_tensor(f"bank{i}", [P, 512], F32)) for i in range(8)]
        s_bank = [bank[0], bank[1]]
        m_bank = [bank[2], bank[3]]
        o_bank = [bank[4], bank[5]]
        r_bank = bank[6]
        t_bank = [bank[4], bank[5]]
        k_bank, q_bank = bank[2], bank[3]
        v_bank = [bank[6], bank[7]]
        h_bank = [bank[0], bank[1]]
        y_bank = [bank[2], bank[3]]
        x_bank = bank[4]

        def f16(b):
            return b[:, :].bitcast(F16)

        weights_in = sem("weights_in")
        x_in = [sem("x_in0"), sem("x_in1")]
        consts = sem("consts")
        waits_settled = sem("waits_settled")
        consts_dve = sem("consts_dve")
        w_hi = sem("w_hi")
        w_lo = sem("w_lo")
        var_ready = sem("var_ready")
        dve_p = sem("dve_p")
        rstd_ready = sem("rstd_ready")
        y_ready = sem("y_ready")
        yhi_ready = sem("yhi_ready")
        ylo_ready = sem("ylo_ready")
        t_done = sem("t_done")
        ythi_ready = sem("ythi_ready")
        ytlo_ready = sem("ytlo_ready")
        k_done = sem("k_done")
        q_done = sem("q_done")
        v_done = sem("v_done")
        khi_ready = sem("khi_ready")
        klo_ready = sem("klo_ready")
        qhi_ready = sem("qhi_ready")
        qlo_ready = sem("qlo_ready")
        v32_ready = sem("v32_ready")
        vhi_ready = sem("vhi_ready")
        vlo_ready = sem("vlo_ready")
        s_done = sem("s_done")
        exp_done = sem("exp_done")
        hi_done = sem("hi_done")
        lo_done = sem("lo_done")
        pv_done = sem("pv_done")
        m_done = sem("m_done")
        m_read = sem("m_read")
        dve_m = sem("dve_m")
        negm_ready = sem("negm_ready")
        row_done = sem("row_done")
        row_ready = sem("row_ready")
        o0_read = sem("o0_read")
        o1_read = sem("o1_read")
        dve_e = sem("dve_e")
        evar_ready = sem("evar_ready")
        erstd_ready = sem("erstd_ready")
        ln_ready = sem("ln_ready")
        pay_ready = sem("pay_ready")
        w_ready = sem("w_ready")
        res_ready = sem("res_ready")
        res_out = sem("res_out")
        dve_r = sem("dve_r")
        cnt_ready = sem("cnt_ready")
        tot_ready = sem("tot_ready")
        rows_ready = sem("rows_ready")
        pack_out = sem("pack_out")
        f_in = [sem(f"f_in{i}") for i in range(RING)]
        thi_ready = sem("thi_ready")
        tlo_ready = sem("tlo_ready")
        ft_done = sem("ft_done")
        tt_ready = sem("tt_ready")
        h_done = sem("h_done")
        gelu_done = sem("gelu_done")
        hhi_ready = sem("hhi_ready")
        hlo_ready = sem("hlo_ready")
        w2_done = sem("w2_done")
        y_read = sem("y_read")
        z_ready = sem("z_ready")
        z_out = [sem(f"z_out{i}") for i in range(RING)]

        E_N = 9
        R_N = 72
        RC_N = 10

        WEIGHTS = 14 * 16
        CONSTS_DVE = 8

        def settled(eng):
            eng.sem_inc(waits_settled, 1)

        block = ctx.enter_context(nc.Block())

        @block.sync
        def _(sp):
            for k, w in enumerate((wq, wk, wv, w1, w2)):
                sp.dma_start(staged[k], w).then_inc(weights_in, 16)
            for s, w in ((bq_s, bq), (bk_s, bk), (br_s, br), (b1_s, b1), (wr_s, wr)):
                sp.dma_start(s[:, :], w).then_inc(weights_in, 16)
            for s, w in ((bv_s, bv), (b2_s, b2)):
                for i in range(2):
                    sp.dma_start(s[:, i, :], w).then_inc(weights_in, 16)

            with sp.Fori(0, B) as b:
                sp.wait_ge(dve_e, b * (NB * E_N) + 3)
                settled(sp)
                with sp.Fori(0, NG // 2) as i:
                    for r in range(2):
                        sp.wait_ge(x_in[r], (b * (NG // 2) + i) * 16 + 16)
                        sp.dma_start(xs[:, bass.ds((i * 2 + r) * GRP, GRP), :],
                                     x_v[bass.ds(b * NG + i * 2 + r, 1)].rearrange("g p t c -> p (g t) c")
                                     ).then_inc(x_in[r], 16)
                with sp.Fori(0, NB) as nb:
                    sp.wait_ge(res_ready, b * NB + nb + 2)
                    sp.dma_start(out_v[bass.ds(b * NB + nb, 1)].rearrange("k p t c -> p (k t) c"),
                                 res[:, :, :]).then_inc(res_out, 16)

            sp.wait_ge(pack_out, B * NT * 16)

            def load_rows(f, ring):
                sp.dma_start(rowb[:, ring, :, :],
                             packed_v[bass.ds(f, 1)].rearrange("f p t c -> p (f t) c")).then_inc(f_in[ring], 16)

            for ring in range(RING):
                load_rows(ring, ring)
            with sp.Fori(1, NI) as i:
                for ring in range(RING):
                    sp.wait_ge(z_out[ring], i * (FT * 16))
                    load_rows(i * RING + ring, ring)
            sp.wait_ge(res_out, B * NB * 16 + 16)
            for ring in range(RING):
                sp.wait_ge(z_out[ring], NI * FT * 16)

        @block.gpsimd
        def _(pool):
            nc.gpsimd.memset(ident[:, :], 0.0).then_inc(consts, 1)
            nc.gpsimd.memset(tri16[:, :], 0.0).then_inc(consts, 1)
            nc.gpsimd.iota(tok[:, :], pattern=[[P, NT]], base=0, channel_multiplier=1).then_inc(consts, 1)
            nc.gpsimd.iota(cand_i[:, :], pattern=[[1, 15]], base=1, channel_multiplier=0).then_inc(consts, 1)
            pool.wait_ge(consts, 4)
            nc.gpsimd.affine_select(out=ident[:, :], in_=ident[:, :], compare_op=ALU.not_equal, fill=1.0,
                                    base=0, pattern=[[-1, P]], channel_multiplier=1).then_inc(consts, 1)
            nc.gpsimd.affine_select(out=tri16[:, :], in_=tri16[:, :], compare_op=ALU.is_ge, fill=1.0,
                                    base=0, pattern=[[-1, P]], channel_multiplier=1).then_inc(consts, 1)

            def project_rstd(g):
                pool.wait_ge(var_ready, g + 1)
                nc.gpsimd.tensor_tensor(rstd[:, :], ve[:, :], mhalf[:, :], ALU.pow).then_inc(rstd_ready, 1)

            def pack_tiles(tiles):
                for t in tiles:
                    nc.gpsimd.indirect_dma_start(
                        out=packed, out_offset=bass.IndirectOffsetOnAxis(ap=rowi[:, t:t + 1].bitcast(U32), axis=0),
                        in_=pay[:, t, :], in_offset=None, bounds_check=ROWS - 1, oob_is_err=False,
                    ).then_inc(pack_out, 16)

            def end_block(k, nb):
                pool.wait_ge(evar_ready, k + 1)
                nc.gpsimd.tensor_tensor(erstd[:, :], eve[:, :], mhalf[:, 0:QT], ALU.pow).then_inc(erstd_ready, 1)
                pool.wait_ge(ln_ready, k * 2 + 2)
                nc.gpsimd.tensor_copy(pay[:, bass.ds(nb * QT, QT), 0:C], lnb[:, :, :]).then_inc(pay_ready, 1)
                pool.wait_ge(res_out, k * 16 + 16)
                nc.gpsimd.tensor_tensor(res[:, :, :], tb[:, :, :], lnb[:, :, :], ALU.add).then_inc(res_ready, 1)

            pool.wait_ge(consts_dve, CONSTS_DVE)
            with pool.Fori(0, NG) as g:
                project_rstd(g)
            pool.wait_ge(w_lo, 5)
            with pool.Fori(0, NB) as nb:
                end_block(nb, nb)
            with pool.Fori(1, B) as b:
                pool.wait_ge(rows_ready, b)
                pool.wait_ge(pay_ready, b * NB)
                for g in range(NG):
                    project_rstd(b * NG + g)
                    pack_tiles(range(g * GRP, (g + 1) * GRP))
                pool.wait_ge(pack_out, b * (NT * 16))
                settled(pool)
                with pool.Fori(0, NB) as nb:
                    end_block(b * NB + nb, nb)
            pool.wait_ge(rows_ready, B)
            pool.wait_ge(pay_ready, B * NB)
            pack_tiles(range(NT))

            pool.wait_ge(res_out, B * NB * 16 + 16)
            with pool.Fori(0, NI) as i:
                for ring in range(RING):
                    pool.wait_ge(z_ready, (i * RING + ring) * FT + FT)
                    settled(pool)
                    for t in range(FT):
                        nc.gpsimd.indirect_dma_start(
                            out=out,
                            out_offset=bass.IndirectOffsetOnAxis(
                                ap=rowb[:, ring, t, C + 1:C + 2].bitcast(U32), axis=0),
                            in_=zb[:, ring, t, :], in_offset=None, bounds_check=B * N - 1, compute_op=ALU.add,
                        ).then_inc(z_out[ring], 16)

        @block.scalar
        def _(act):
            act.wait_ge(weights_in, WEIGHTS)
            for s, w in zip(staged, split):
                nc.scalar.copy(w[:, 0, :], s).then_inc(w_hi, 1)

            def y_hi(g):
                act.wait_ge(y_ready, g * GRP + GRP)
                act.wait_ge(t_done, g + 1)
                nc.scalar.copy(yhl[:, 0, :, :], y32[:, :, :]).then_inc(yhi_ready, 1)

            def yt_hi(g):
                act.wait_ge(t_done, g + 2)
                act.wait_ge(v_done, g * 2 + 2)
                nc.scalar.copy(yt[:, 0, :, :].rearrange("p c n -> p (c n)"), f16(t_bank[0])).then_inc(ythi_ready, 1)

            def qkv_hi(gi, g):
                cols = bass.ds(g * GW, GW)
                act.wait_ge(k_done, gi + 1)
                nc.scalar.activation(ka[:, cols], k_bank[:, :], ACT.Identity, bias=bk_s[:, 0:1]
                                     ).then_inc(khi_ready, 1)
                act.wait_ge(q_done, gi + 1)
                nc.scalar.activation(qb[:, cols], q_bank[:, :], ACT.Identity, bias=bq_s[:, 0:1])
                nc.scalar.activation(qa[0:D, cols], q_bank[0:D, :], ACT.Identity, bias=bq_s[0:D, 0:1]
                                     ).then_inc(qhi_ready, 1)
                for h in range(2):
                    act.wait_ge(v32_ready, gi * 2 + h + 3)
                    nc.scalar.copy(vs[:, bass.ds(g * GRP + h * 2, 2), 0:C], v32[:, h, :, :]).then_inc(vhi_ready, 1)

            def exponent(t, j):
                act.wait_ge(s_done, t + 1)
                act.wait_ge(lo_done, t + 1)
                nc.scalar.activation(p32[:, j % 2, :, :].rearrange("p m n -> p (m n)"), s_bank[j % 2][:, :],
                                     ACT.Exp).then_inc(exp_done, 1)

            def p_hi(t, j):
                act.wait_ge(exp_done, t + 3)
                act.wait_ge(pv_done, t + 1)
                nc.scalar.copy(phi[:, j % 4, :, :], p32[:, j % 2, :, :]).then_inc(hi_done, 1)

            def evacuate(k):
                act.wait_ge(pv_done, k * STEPS + STEPS + 4)
                nc.scalar.copy(oe[:, 1, :], o_bank[1][:, 0:C + 1]).then_inc(o1_read, 1)

            def row(k, nb):
                act.wait_ge(row_done, k + 1)
                nc.scalar.copy(qb[D:D + 1, bass.ds(nb * QB, QB)], r_bank[D:D + 1, 0:QB]).then_inc(row_ready, 1)

            def attend(k, nb, first, last):
                for j in range(STEPS):
                    t = k * STEPS + j
                    p_hi(t, j)
                    if j + 1 < STEPS or not last:
                        exponent(t + 1, j + 1)
                    if j == 0 and not first:
                        evacuate(k - 1)
                    if j == 12 and not last:
                        row(k + 1, nb + 1)

            with act.Fori(0, B) as b:
                g0 = b * NG
                y_hi(g0)
                yt_hi(g0)
                with act.Fori(0, NG - 1) as g:
                    y_hi(g0 + g + 1)
                    qkv_hi(g0 + g, g)
                    yt_hi(g0 + g + 1)
                qkv_hi(g0 + NG - 1, NG - 1)
                k0 = b * NB
                row(k0, 0)
                exponent(k0 * STEPS, 0)
                attend(k0, 0, True, False)
                with act.Fori(1, NB - 1) as nb:
                    attend(k0 + nb, nb, False, False)
                attend(k0 + NB - 1, NB - 1, False, True)
                evacuate(k0 + NB - 1)

            def row_hi(f, ring, i):
                act.wait_ge(f_in[ring], i * 16 + 16)
                act.wait_ge(ft_done, f + 1)
                nc.scalar.copy(thl[:, 0, :, :], rowb[:, ring, :, 0:C]).then_inc(thi_ready, 1)

            def mlp(f, ring, i, last):
                for p in range(HC // 2):
                    q = f * (HC // 2) + p
                    act.wait_ge(h_done, q + 1)
                    act.wait_ge(hlo_ready, q + 1)
                    nc.scalar.activation(h32[:, p % 2, 0, :], h_bank[p % 2][:, 0:FB], ACT.Gelu_apprx_tanh,
                                         bias=b1_s[:, 2 * p:2 * p + 1])
                    nc.scalar.activation(h32[:, p % 2, 1, :], h_bank[p % 2][:, FB:2 * FB], ACT.Gelu_apprx_tanh,
                                         bias=b1_s[:, 2 * p + 1:2 * p + 2]).then_inc(gelu_done, 1)
                    act.wait_ge(gelu_done, q + 3)
                    act.wait_ge(w2_done, q + 1)
                    nc.scalar.copy(hhi[:, p % 2, :, :], h32[:, p % 2, :, :]).then_inc(hhi_ready, 1)
                    if p == 0 and not last:
                        row_hi(f + 1, (ring + 1) % RING, i + (ring + 1) // RING)

            row_hi(0, 0, 0)
            with act.Fori(0, NI - 1) as i:
                for ring in range(RING):
                    mlp(i * RING + ring, ring, i, False)
            for ring in range(RING):
                mlp(NF - RING + ring, ring, NI - 1, ring == RING - 1)

        @block.vector
        def _(dve):
            V = nc.vector
            for s, n in ((x_in[0], 16), (x_in[1], 16), (yhi_ready, 1), (t_done, 1), (klo_ready, 1), (qlo_ready, 1),
                         (v32_ready, 2), (v_done, 2), (exp_done, 2), (lo_done, 2), (pv_done, 4), (m_read, 2),
                         (o0_read, 1), (o1_read, 1), (dve_e, E_N), (res_ready, 1), (res_out, 16), (ft_done, 1),
                         (tt_ready, 1), (gelu_done, 2), (hlo_ready, 2), (w2_done, 2), (y_read, 2)):
                dve.sem_inc(s, n)
            V.memset(ones16[:, :], 1.0).then_inc(consts_dve, 1)
            V.memset(vs[:, :, C:C + 1], 1.0).then_inc(consts_dve, 1)
            V.memset(kb[D:D + 1, :], 1.0).then_inc(consts_dve, 1)
            V.memset(mhalf[:, :], -0.5).then_inc(consts_dve, 1)
            V.memset(zeros[:, :], 0.0).then_inc(consts_dve, 1)
            V.memset(rbase[:, :], 0.0).then_inc(consts_dve, 1)
            dve.wait_ge(consts, 6)
            V.tensor_copy(cand1[:, :], cand_i[:, :]).then_inc(consts_dve, 1)
            V.tensor_copy(tokf[:, :], tok[:, :]).then_inc(consts_dve, 1)
            for n, (s, w) in enumerate(zip(staged, split)):
                dve.wait_ge(w_hi, n + 1)
                V.tensor_tensor(w[:, 1, :], s, w[:, 0, :], ALU.subtract).then_inc(w_lo, 1)

            def normalise(gi, g, r):
                dve.wait_ge(x_in[r], (gi - r) * 8 + 32)
                p0 = gi * (2 * GRP)
                for t in range(GRP):
                    V.bn_stats(st[:, t, :], xs[:, bass.ds(g * GRP + t, 1), :].rearrange("p a c -> p (a c)")
                               ).then_inc(dve_p, 1)
                dve.wait_ge(dve_p, p0 + GRP)
                settled(dve)
                for t in range(GRP):
                    V.bn_aggr(mv[:, t, :], st[:, t, :]).then_inc(dve_p, 1)
                dve.wait_ge(dve_p, p0 + 2 * GRP)
                V.tensor_scalar(ve[:, :], mv[:, :, 1], 1e-6, None, ALU.add).then_inc(var_ready, 1)
                dve.wait_ge(rstd_ready, gi + 1)
                dve.wait_ge(yhi_ready, gi + 1)
                for t in range(GRP):
                    V.tensor_scalar(y32[:, t, :], xs[:, bass.ds(g * GRP + t, 1), :].rearrange("p a c -> p (a c)"),
                                    mv[:, t, 0:1], rstd[:, t:t + 1], ALU.subtract, ALU.mult).then_inc(y_ready, 1)
                dve.wait_ge(yhi_ready, gi + 2)
                V.tensor_tensor(yhl[:, 1, :, :], y32[:, :, :], yhl[:, 0, :, :], ALU.subtract).then_inc(ylo_ready, 1)

            def yt_lo(gi):
                dve.wait_ge(t_done, gi + 2)
                dve.wait_ge(v_done, gi * 2 + 2)
                V.tensor_copy(yt[:, 1, :, :].rearrange("p c n -> p (c n)"), f16(t_bank[1])).then_inc(ytlo_ready, 1)

            def qkv_lo(gi, g):
                cols = bass.ds(g * GW, GW)
                dve.wait_ge(khi_ready, gi + 1)
                V.scalar_tensor_tensor(out=kb[0:D, cols], in0=k_bank[0:D, :], scalar=bk_s[0:D, 0:1],
                                       in1=ka[0:D, cols], op0=ALU.add, op1=ALU.subtract).then_inc(klo_ready, 1)
                dve.wait_ge(qhi_ready, gi + 1)
                V.scalar_tensor_tensor(out=qa[D:2 * D, cols], in0=q_bank[D:2 * D, :], scalar=bq_s[D:2 * D, 0:1],
                                       in1=qb[D:2 * D, cols], op0=ALU.add, op1=ALU.subtract).then_inc(qlo_ready, 1)
                for h in range(2):
                    dve.wait_ge(v_done, gi * 2 + h + 3)
                    V.tensor_tensor(v32[:, h, :, :], v_bank[h][:, :].rearrange("p (t c) -> p t c", t=2),
                                    bv_s[:, :, :], ALU.add).then_inc(v32_ready, 1)
                for h in range(2):
                    dve.wait_ge(vhi_ready, gi * 2 + h + 1)
                    tiles = bass.ds(g * GRP + h * 2, 2)
                    V.tensor_tensor(vs[:, tiles, VLO:VLO + C], v32[:, h, :, :], vs[:, tiles, 0:C],
                                    ALU.subtract).then_inc(vlo_ready, 1)

            def p_lo(t, j):
                dve.wait_ge(hi_done, t + 1)
                V.tensor_tensor(plo[:, j % 4, :, :], p32[:, j % 2, :, :], phi[:, j % 4, :, :],
                                ALU.subtract).then_inc(lo_done, 1)

            def unit_max(k, u):
                dve.wait_ge(m_done, k * UNITS + u + 1)
                V.tensor_reduce(mpart[:, u // 8, u % 8:u % 8 + 1], m_bank[u % 2][:, :], AX.X, ALU.max
                                ).then_inc(m_read, 1)

            def row_max(k):
                dve.wait_ge(m_read, k * UNITS + UNITS + 2)
                V.tensor_reduce(mrow[:, :], mpart[:, :, :], AX.X, ALU.max).then_inc(dve_m, 1)
                dve.wait_ge(dve_m, k + 1)
                V.tensor_scalar(negm[:, :], mrow[:, :], -1.0, SHIFT, ALU.mult, ALU.add).then_inc(negm_ready, 1)

            def end_block(k, nb, part):
                e0 = k * E_N + E_N
                if part == 0:
                    dve.wait_ge(pv_done, k * STEPS + STEPS + 4)
                    V.tensor_copy(oe[:, 0, :], o_bank[0][:, 0:C + 1]).then_inc(o0_read, 1)
                elif part == 1:
                    dve.wait_ge(o0_read, k + 2)
                    dve.wait_ge(o1_read, k + 2)
                    V.reciprocal(rz[:, :], oe[:, :, C]).then_inc(dve_e, 1)
                elif part == 2:
                    dve.wait_ge(dve_e, e0 + 1)
                    dve.wait_ge(res_ready, k + 1)
                    for i in range(QT):
                        V.scalar_tensor_tensor(out=tb[:, i, :], in0=oe[:, i, 0:C], scalar=rz[:, i:i + 1],
                                               in1=xs[:, bass.ds(nb * QT + i, 1), :].rearrange("p a c -> p (a c)"),
                                               op0=ALU.mult, op1=ALU.add).then_inc(dve_e, 1)
                elif part == 3:
                    dve.wait_ge(dve_e, e0 + 3)
                    for i in range(QT):
                        V.bn_stats(est[:, i, :], tb[:, i, :]).then_inc(dve_e, 1)
                elif part == 4:
                    dve.wait_ge(dve_e, e0 + 5)
                    settled(dve)
                    for i in range(QT):
                        V.bn_aggr(emv[:, i, :], est[:, i, :]).then_inc(dve_e, 1)
                    dve.wait_ge(dve_e, e0 + 7)
                    V.tensor_scalar(eve[:, :], emv[:, :, 1], 1e-5, None, ALU.add).then_inc(evar_ready, 1)
                elif part == 5:
                    dve.wait_ge(erstd_ready, k + 1)
                    for i in range(QT):
                        V.tensor_scalar(lnb[:, i, :], tb[:, i, :], emv[:, i, 0:1], erstd[:, i:i + 1],
                                        ALU.subtract, ALU.mult).then_inc(ln_ready, 1)
                elif part == 6:
                    dve.wait_ge(ln_ready, k * 2 + 2)
                    for i in range(QT):
                        V.tensor_tensor_reduce(out=wjunk[:, i, :], in0=lnb[:, i, :], in1=wr_s[:, :], scale=1.0,
                                               scalar=0.0, op0=ALU.mult, op1=ALU.add, accum_out=wdot[:, i:i + 1]
                                               ).then_inc(dve_e, 1)
                elif part == 7:
                    dve.wait_ge(dve_e, e0 + 9)
                    V.tensor_scalar(wcol[:, bass.ds(nb * QT, QT)], wdot[:, :], br_s[:, 0:1], None, ALU.add
                                    ).then_inc(w_ready, 1)

            PART_AT = {0: 0, 1: 1, 2: 2, 3: 3, 4: 4, 6: 5, 7: 6, 8: 7}

            def attend(k, nb, first, last):
                u = 0
                for j in range(STEPS):
                    p_lo(k * STEPS + j, j)
                    if j in PART_AT and not first:
                        end_block(k - 1, nb - 1, PART_AT[j])
                    if not last:
                        for _ in range(UNIT_OF[j]):
                            unit_max(k + 1, u)
                            u += 1
                        if UNIT_OF[j] and u == UNITS:
                            row_max(k + 1)

            def route(b):
                n = [0]

                def own(ins):
                    ins.then_inc(dve_r, 1)
                    n[0] += 1
                    dve.wait_ge(dve_r, b * R_N + n[0])

                events = [0]

                def sums():
                    events[0] += 1
                    dve.wait_ge(tot_ready, b * RC_N + events[0])

                def search(vals, col):
                    own(V.memset(base[:, col:col + 1], 0.0))
                    for step in (4096.0, 256.0, 16.0, 1.0):
                        own(V.tensor_scalar(cand[:, :], cand1[:, :], step, base[:, col:col + 1], ALU.mult, ALU.add))
                        own(V.tensor_tensor(cmp[:, :, :], vals[:, :].unsqueeze(1).to_broadcast([P, 15, NT]),
                                            cand[:, :].unsqueeze(2).to_broadcast([P, 15, NT]), ALU.is_ge))
                        with nc.allow_low_precision(reason="counts up to 32 are exact"):
                            V.tensor_reduce(cnt[:, :], cmp[:, :, :], AX.X, ALU.add).then_inc(cnt_ready, 1)
                        sums()
                        own(V.tensor_scalar(isge[:, :], r_bank[:, 0:15], KEEP - 0.5, None, ALU.is_ge))
                        own(V.tensor_reduce(nge[:, :], isge[:, :], AX.X, ALU.add))
                        own(V.scalar_tensor_tensor(out=base[:, col:col + 1], in0=nge[:, :], scalar=step,
                                                   in1=base[:, col:col + 1], op0=ALU.mult, op1=ALU.add))

                def rank_of(col_sums, prefix):
                    own(V.tensor_tensor_scan(csum[:, :], zeros[:, :], col_sums, 0.0, ALU.add, ALU.add))
                    own(V.tensor_tensor(cexc[:, :], csum[:, :], col_sums, ALU.subtract))
                    own(V.tensor_tensor(rank[:, :], cexc[:, :], prefix, ALU.add))

                dve.wait_ge(w_ready, b * NB + NB)
                w_i = wcol[:, :].bitcast(I32)
                own(V.tensor_scalar(keym[:, :], w_i, 31, -2147483648, ALU.arith_shift_right, ALU.bitwise_or))
                own(V.tensor_tensor(key[:, :], w_i, keym[:, :], ALU.bitwise_xor))
                own(V.tensor_scalar(kpart[:, :].bitcast(U32), key[:, :].bitcast(U32), 16, None,
                                    ALU.logical_shift_right))
                own(V.tensor_copy(khi[:, :], kpart[:, :]))
                own(V.tensor_scalar(kpart[:, :], key[:, :], 65535, None, ALU.bitwise_and))
                own(V.tensor_copy(klo[:, :], kpart[:, :]))
                search(khi, 0)
                own(V.tensor_scalar(vtmp[:, :], klo[:, :], 1.0, None, ALU.add))
                own(V.scalar_tensor_tensor(out=vtmp[:, :], in0=khi[:, :], scalar=base[:, 0:1], in1=vtmp[:, :],
                                           op0=ALU.is_equal, op1=ALU.mult))
                own(V.tensor_scalar(val[:, :], khi[:, :], base[:, 0:1], 70000.0, ALU.is_gt, ALU.mult))
                own(V.scalar_tensor_tensor(out=val[:, :], in0=val[:, :], scalar=-1.0, in1=vtmp[:, :],
                                           op0=ALU.add, op1=ALU.add))
                search(val, 1)
                own(V.tensor_scalar(gt16[:, :], val[:, :], base[:, 1:2], None, ALU.is_gt))
                V.tensor_scalar(eq16[:, :], val[:, :], base[:, 1:2], None, ALU.is_equal).then_inc(cnt_ready, 1)
                sums()
                own(V.tensor_reduce(ngt[:, :], r_bank[:, 0:NT], AX.X, ALU.add))
                own(V.tensor_scalar(need[:, :], ngt[:, :], -1.0, float(KEEP), ALU.mult, ALU.add))
                rank_of(r_bank[:, NT:2 * NT], r_bank[:, 2 * NT:3 * NT])
                own(V.scalar_tensor_tensor(out=take[:, :], in0=rank[:, :], scalar=need[:, 0:1], in1=eq16[:, :],
                                           op0=ALU.is_lt, op1=ALU.mult))
                own(V.tensor_scalar(drop[:, :], rank[:, :], 1.0, need[:, 0:1], ALU.add, ALU.is_equal))
                own(V.tensor_tensor(drop[:, :], drop[:, :], eq16[:, :], ALU.mult))
                own(V.tensor_scalar(drop[:, :], drop[:, :], -1.0, 1.0, ALU.mult, ALU.add))
                V.tensor_tensor(sel16[:, :], take[:, :], gt16[:, :], ALU.add).then_inc(cnt_ready, 1)
                own(V.tensor_tensor(pay[:, :, C], wcol[:, :], drop[:, :], ALU.mult))
                own(V.tensor_copy(pay[:, :, C + 1].bitcast(I32), tokf[:, :]))
                own(V.tensor_scalar(tokf[:, :], tokf[:, :], float(N), None, ALU.add))
                sums()
                rank_of(r_bank[:, 0:NT], r_bank[:, NT:2 * NT])
                own(V.scalar_tensor_tensor(out=rowf[:, :], in0=rank[:, :], scalar=rbase[:, 0:1], in1=sel16[:, :],
                                           op0=ALU.add, op1=ALU.mult))
                own(V.tensor_scalar(take[:, :], sel16[:, :], -BIG, BIG, ALU.mult, ALU.add))
                own(V.tensor_tensor(rowf[:, :], rowf[:, :], take[:, :], ALU.add))
                own(V.tensor_scalar(rbase[:, :], rbase[:, :], float(KEEP), None, ALU.add))
                V.tensor_copy(rowi[:, :], rowf[:, :]).then_inc(rows_ready, 1)
                assert n[0] == R_N and events[0] == RC_N, (n[0], events[0])

            with dve.Fori(0, B) as b:
                g0 = b * NG
                normalise(g0, 0, 0)
                yt_lo(g0)
                with dve.Fori(0, NG // 2 - 1) as i:
                    for r in range(2):
                        normalise(g0 + i * 2 + r + 1, i * 2 + r + 1, 1 - r)
                        qkv_lo(g0 + i * 2 + r, i * 2 + r)
                        yt_lo(g0 + i * 2 + r + 1)
                normalise(g0 + NG - 1, NG - 1, 1)
                qkv_lo(g0 + NG - 2, NG - 2)
                yt_lo(g0 + NG - 1)
                qkv_lo(g0 + NG - 1, NG - 1)
                k0 = b * NB
                for u in range(UNITS):
                    unit_max(k0, u)
                row_max(k0)
                attend(k0, 0, True, False)
                with dve.Fori(1, NB - 1) as nb:
                    attend(k0 + nb, nb, False, False)
                attend(k0 + NB - 1, NB - 1, False, True)
                for part in range(8):
                    end_block(k0 + NB - 1, NB - 1, part)
                route(b)

            def row_lo(f, ring):
                dve.wait_ge(thi_ready, f + 1)
                V.tensor_tensor(thl[:, 1, :, :], rowb[:, ring, :, 0:C], thl[:, 0, :, :], ALU.subtract
                                ).then_inc(tlo_ready, 1)

            def rows_t(f, ring):
                dve.wait_ge(ft_done, f + 2)
                V.tensor_copy(tt[:, ring % 2, :, :, :].rearrange("p h c n -> p (h c n)"), f16(x_bank)
                              ).then_inc(tt_ready, 1)

            def finish(f, ring):
                dve.wait_ge(w2_done, f * 4 + 6)
                V.tensor_tensor(yb[:, :, :], y_bank[ring % 2][:, :].rearrange("p (t c) -> p t c", t=FT), b2_s[:, :, :],
                                ALU.add).then_inc(y_read, 1)
                dve.wait_ge(y_read, f + 3)
                for t in range(FT):
                    V.tensor_scalar(zb[:, ring, t, :], yb[:, t, :], rowb[:, ring, t, C:C + 1], None, ALU.mult
                                    ).then_inc(z_ready, 1)

            def mlp(f, ring, first, last):
                for p in range(HC // 2):
                    dve.wait_ge(hhi_ready, f * 4 + p + 1)
                    V.tensor_tensor(hlo[:, p % 2, :, :], h32[:, p % 2, :, :], hhi[:, p % 2, :, :], ALU.subtract
                                    ).then_inc(hlo_ready, 1)
                    if p == 0 and not last:
                        row_lo(f + 1, (ring + 1) % RING)
                    if p == 1 and not first:
                        finish(f - 1, (ring - 1) % RING)
                    if p == 2 and not last:
                        rows_t(f + 1, (ring + 1) % RING)

            row_lo(0, 0)
            rows_t(0, 0)
            for ring in range(RING):
                mlp(ring, ring, ring == 0, False)
            with dve.Fori(1, NI - 1) as i:
                for ring in range(RING):
                    mlp(i * RING + ring, ring, False, False)
            for ring in range(RING):
                mlp(NF - RING + ring, ring, False, ring == RING - 1)
            finish(NF - 1, RING - 1)

        @block.tensor
        def _(pe):
            mm = nc.tensor.matmul
            pe.wait_ge(w_lo, 5)
            pe.wait_ge(consts, 6)
            pe.wait_ge(consts_dve, CONSTS_DVE)
            TERMS = ((0, 0), (0, 1), (1, 0))

            def transpose_y(gi):
                pe.wait_ge(ylo_ready, gi + 1)
                for h in range(2):
                    for c in range(CC):
                        for t in range(GRP):
                            last = nc.tensor.transpose(f16(t_bank[h])[:, c * GW + t * P:c * GW + (t + 1) * P],
                                                       yhl[:, h, t, c * P:(c + 1) * P], ident[:, :])
                last.then_inc(t_done, 1)

            def project(gi):
                pe.wait_ge(ythi_ready, gi + 1)
                pe.wait_ge(ytlo_ready, gi + 1)
                for w, bk_, free, done in ((wk_s, k_bank, klo_ready, k_done), (wq_s, q_bank, qlo_ready, q_done)):
                    pe.wait_ge(free, gi + 1)
                    for n, (a, c2) in enumerate(TERMS):
                        for c in range(CC):
                            last = mm(bk_[:, :], w[:, a, c, :], yt[:, c2, c, :], start=(n == 0 and c == 0),
                                      stop=(n == 2 and c == CC - 1))
                    last.then_inc(done, 1)
                pe.wait_ge(v32_ready, gi * 2 + 2)
                for h in range(2):
                    for t in range(2):
                        tok_cols = slice((h * 2 + t) * P, (h * 2 + t + 1) * P)
                        for n, (a, c2) in enumerate(TERMS):
                            for c in range(CC):
                                last = mm(v_bank[h][:, t * C:(t + 1) * C], yt[:, a, c, tok_cols], wv_s[:, c2, c, :],
                                          start=(n == 0 and c == 0), stop=(n == 2 and c == CC - 1))
                    last.then_inc(v_done, 1)

            def scores(t, nb, j):
                pe.wait_ge(exp_done, t + 1)
                cols = bass.ds(nb * QB, QB)
                for m in range(2):
                    keys = slice((2 * j + m) * P, (2 * j + m + 1) * P)
                    o = s_bank[j % 2][:, m * QB:(m + 1) * QB]
                    mm(o, ka[:, keys], qa[:, cols], start=True, stop=False)
                    last = mm(o, kb[0:D + 1, keys], qb[0:D + 1, cols], start=False, stop=True)
                last.then_inc(s_done, 1)

            def unit(k, nb, u):
                pe.wait_ge(m_read, k * UNITS + u + 1)
                mm(m_bank[u % 2][:, :], qa[:, bass.ds(nb * QB + (u // 8) * P, P)],
                   ka[:, (u % 8) * 512:(u % 8 + 1) * 512], start=True, stop=True).then_inc(m_done, 1)

            def max_row(k):
                pe.wait_ge(negm_ready, k + 1)
                for i in range(QT):
                    last = mm(r_bank[D:D + 1, i * P:(i + 1) * P], negm[:, i:i + 1], ident[:, :], start=True, stop=True)
                last.then_inc(row_done, 1)

            def p_v(t, j):
                pe.wait_ge(lo_done, t + 3)
                for m in range(2):
                    v_hi1 = vs[:, 2 * j + m, 0:C + 1]
                    v_lo = vs[:, 2 * j + m, VLO:VLO + C]
                    for i in range(QT):
                        ph = phi[:, j % 4, m, i * P:(i + 1) * P]
                        pl = plo[:, j % 4, m, i * P:(i + 1) * P]
                        begin, end = j == 0 and m == 0, j == STEPS - 1 and m == 1
                        mm(o_bank[i][:, 0:C + 1], ph, v_hi1, start=begin, stop=False, skip_group_check=True)
                        mm(o_bank[i][:, 0:C], ph, v_lo, start=False, stop=False, skip_group_check=True)
                        last = mm(o_bank[i][:, 0:C + 1], pl, v_hi1, start=False, stop=end, skip_group_check=True)
                last.then_inc(pv_done, 1)

            def attend(k, nb, last):
                u = 0
                for j in range(STEPS):
                    t = k * STEPS + j
                    if j + 2 < STEPS:
                        scores(t + 2, nb, j + 2)
                    elif not last:
                        if j == STEPS - 2:
                            pe.wait_ge(row_ready, k + 2)
                        scores(t + 2, nb + 1, j + 2 - STEPS)
                    if not last:
                        for _ in range(UNIT_OF[j]):
                            unit(k + 1, nb + 1, u)
                            u += 1
                    if j == 0:
                        pe.wait_ge(o0_read, k + 1)
                        pe.wait_ge(o1_read, k + 1)
                    p_v(t, j)
                    if j == 12 and not last:
                        max_row(k + 1)

            def route(b):
                for e in range(RC_N):
                    pe.wait_ge(cnt_ready, b * RC_N + e + 1)
                    if e < 8:
                        last = mm(r_bank[:, 0:15], ones16[:, :], cnt[:, :], start=True, stop=True)
                    elif e == 8:
                        mm(r_bank[:, 0:NT], ones16[:, :], gt16[:, :], start=True, stop=True)
                        mm(r_bank[:, NT:2 * NT], ones16[:, :], eq16[:, :], start=True, stop=True)
                        last = mm(r_bank[:, 2 * NT:3 * NT], tri16[:, :], eq16[:, :], start=True, stop=True)
                    else:
                        mm(r_bank[:, 0:NT], ones16[:, :], sel16[:, :], start=True, stop=True)
                        last = mm(r_bank[:, NT:2 * NT], tri16[:, :], sel16[:, :], start=True, stop=True)
                    last.then_inc(tot_ready, 1)

            with pe.Fori(0, B) as b:
                g0 = b * NG
                pe.wait_ge(o0_read, b * NB + 1)
                pe.wait_ge(o1_read, b * NB + 1)
                transpose_y(g0)
                with pe.Fori(0, NG - 1) as g:
                    project(g0 + g)
                    transpose_y(g0 + g + 1)
                project(g0 + NG - 1)
                pe.wait_ge(klo_ready, g0 + NG + 1)
                pe.wait_ge(qlo_ready, g0 + NG + 1)
                pe.wait_ge(vlo_ready, g0 * 2 + NG * 2)
                k0 = b * NB
                for u in range(UNITS):
                    unit(k0, 0, u)
                max_row(k0)
                pe.wait_ge(row_ready, k0 + 1)
                for j in range(2):
                    scores(k0 * STEPS + j, 0, j)
                attend(k0, 0, False)
                with pe.Fori(1, NB - 1) as nb:
                    attend(k0 + nb, nb, False)
                attend(k0 + NB - 1, NB - 1, True)
                route(b)

            def transpose_rows(f):
                pe.wait_ge(tlo_ready, f + 1)
                pe.wait_ge(tt_ready, f + 1)
                for h in range(2):
                    for c in range(CC):
                        for t in range(FT):
                            at = (h * CC + c) * FB + t * P
                            last = nc.tensor.transpose(f16(x_bank)[:, at:at + P], thl[:, h, t, c * P:(c + 1) * P],
                                                       ident[:, :])
                last.then_inc(ft_done, 1)

            def hidden(f, ring, p):
                if p == 0:
                    pe.wait_ge(tt_ready, f + 2)
                pe.wait_ge(gelu_done, f * 4 + p + 1)
                for hh in range(2):
                    units = slice((2 * p + hh) * P, (2 * p + hh + 1) * P)
                    for n, (a, c2) in enumerate(TERMS):
                        for c in range(CC):
                            last = mm(h_bank[p % 2][:, hh * FB:(hh + 1) * FB], w1_s[:, a, c, units],
                                      tt[:, ring % 2, c2, c, :], start=(n == 0 and c == 0), stop=(n == 2 and c == CC - 1))
                last.then_inc(h_done, 1)

            def second(f, ring, p):
                pe.wait_ge(hlo_ready, f * 4 + p + 3)
                if p == 0:
                    pe.wait_ge(y_read, f + 1)
                for hh in range(2):
                    for t in range(FT):
                        o = y_bank[ring % 2][:, t * C:(t + 1) * C]
                        for n, (a, c2) in enumerate(TERMS):
                            h = (hhi, hlo)[a][:, p % 2, hh, t * P:(t + 1) * P]
                            last = mm(o, h, w2_s[:, c2, 2 * p + hh, :], start=(p == hh == t == n == 0),
                                      stop=(p == 3 and hh == 1 and n == 2), skip_group_check=True)
                last.then_inc(w2_done, 1)

            def mlp(f, ring, last):
                for p in range(HC // 2):
                    if p + 1 < HC // 2:
                        hidden(f, ring, p + 1)
                    elif not last:
                        hidden(f + 1, ring + 1, 0)
                    second(f, ring, p)
                    if p == 1 and not last:
                        transpose_rows(f + 1)

            pe.wait_ge(o0_read, B * NB + 1)
            pe.wait_ge(o1_read, B * NB + 1)
            transpose_rows(0)
            hidden(0, 0, 0)
            with pe.Fori(0, NI - 1) as i:
                for ring in range(RING):
                    mlp(i * RING + ring, ring, False)
            for ring in range(RING):
                mlp(NF - RING + ring, ring, ring == RING - 1)


def kernel(**inputs):
    import numpy as np
    import concourse.bacc as bacc
    from concourse.bass_utils import run_bass_kernel_spmd

    a = {k: np.asarray(v) for k, v in inputs.items()}
    wide = lambda v, n: np.ascontiguousarray(np.broadcast_to(v.reshape(1, -1), (P, n)))

    def by_rows(w):
        k, n = w.shape
        return np.ascontiguousarray(w.reshape(k // P, P, n).transpose(1, 0, 2).reshape(P, -1))

    def twice(v):
        return np.ascontiguousarray(np.concatenate([v, v], axis=-1))

    arrays = {
        "x": np.ascontiguousarray(a["x"].reshape(B, C, N).transpose(0, 2, 1).reshape(B * N, C)),
        "wq": by_rows(twice(a["L0_conv_wq"].T)),
        "wk": by_rows(twice(a["L0_conv_wk"].T)),
        "wv": by_rows(a["L0_conv_wv"].T),
        "bq": twice(a["L0_conv_bq"]).reshape(P, 1),
        "bk": twice(a["L0_conv_bk"]).reshape(P, 1),
        "bv": wide(a["L0_conv_bv"], C),
        "wr": wide(a["L0_ffn_wr"], C),
        "br": wide(a["L0_ffn_br"], 1),
        "w1": by_rows(a["L0_ffn_w1"]),
        "b1": np.ascontiguousarray(a["L0_ffn_b1"].reshape(HC, P).T),
        "w2": by_rows(a["L0_ffn_w2"]),
        "b2": wide(a["L0_ffn_b2"], C),
    }
    nc = bacc.Bacc("TRN2", target_bir_lowering=False, num_devices=1)
    args = {k: nc.dram_tensor(f"in_{k}", v.shape, F32, kind="ExternalInput").ap() for k, v in arrays.items()}
    args["out"] = nc.dram_tensor("out_rows", (B * N, C), F32, kind="ExternalOutput").ap()
    build(nc, **args)
    r = run_bass_kernel_spmd(nc, [{f"in_{k}": v for k, v in arrays.items()}], core_ids=[0])
    rows = r.results[0]["out_rows"]
    return np.ascontiguousarray(rows.reshape(B, N, C).transpose(0, 2, 1)).reshape(B, C, 64, 64)
```

```python
from contextlib import ExitStack

import concourse.bass as bass
from concourse import mybir

F32 = mybir.dt.float32
F16 = mybir.dt.float16
I32 = mybir.dt.int32
U32 = mybir.dt.uint32
ALU = mybir.AluOpType
ACT = mybir.ActivationFunctionType
AX = mybir.AxisListType

P = 128
B = 4
N = 4096
C = 256
D = 64
HID = 1024
CC = C // P
HC = HID // P
NT = N // P
KEEP = N // 2
QB = 256
QT = QB // P
NB = N // QB
BLOCKS = B * NB
AHEAD = NB + 1
STEPS = NT // 2
UNITS = QT * (N // 512)
VW = 514
VLO = 258
ROWS = B * KEEP
FB = 256
FT = FB // P
NF = ROWS // FB
RING = 4
NI = NF // RING
SHIFT = 6.0
UNIT_OF = [1, 2, 1, 1, 1, 2, 1, 1, 2, 1, 1, 1, 1, 0, 0, 0]
assert sum(UNIT_OF) == UNITS and len(UNIT_OF) == STEPS
BIG = 100000.0


def build(nc, x, wq, wk, wv, bq, bk, bv, wr, br, w1, b1, w2, b2, out):
    ctx = ExitStack()
    with ctx:
        def sb(name, shape, dt):
            return ctx.enter_context(nc.sbuf_tensor(name, shape, dt))

        def sem(name):
            return ctx.enter_context(nc.semaphore(name))

        packed = nc.dram_tensor("packed", (ROWS, 2), F32, kind="Internal").ap()
        ln_rows = nc.dram_tensor("ln_rows", (B * N, C), F32, kind="Internal").ap()
        x_v = x.rearrange("(k t p) c -> k p t c", p=P, t=QT)
        out_v = out.rearrange("(k t p) c -> k p t c", p=P, t=QT)
        ln_v = ln_rows.rearrange("(k t p) c -> k p t c", p=P, t=QT)
        packed_v = packed.rearrange("(f t p) c -> f p t c", p=P, t=FT)

        ident = sb("ident", [P, P], F16)
        ones16 = sb("ones16", [P, P], F16)
        tri16 = sb("tri16", [P, P], F16)
        wq_s = sb("wq_s", [P, 2, CC, P], F16)
        wk_s = sb("wk_s", [P, 2, CC, P], F16)
        wv_s = sb("wv_s", [P, 2, CC, C], F16)
        w1_s = sb("w1_s", [P, 2, CC, HID], F16)
        w2_s = sb("w2_s", [P, 2, HC, C], F16)
        bq_s = sb("bq_s", [P, 1], F32)
        bk_s = sb("bk_s", [P, 1], F32)
        br_s = sb("br_s", [P, 1], F32)
        b1_s = sb("b1_s", [P, HC], F32)
        bv_s = sb("bv_s", [P, QT, C], F32)
        wr_s = sb("wr_s", [P, C], F32)
        b2_s = sb("b2_s", [P, FT, C], F32)
        ka = [sb(f"ka{i}", [P, N], F16) for i in range(2)]
        kb = [sb(f"kb{i}", [P, N], F16) for i in range(2)]
        qa = [sb(f"qa{i}", [P, N], F16) for i in range(2)]
        qb = [sb(f"qb{i}", [P, N], F16) for i in range(2)]
        vs = [sb(f"vs{i}", [P, NT, VW], F16) for i in range(2)]
        xp = sb("xp", [P, QT, C], F32)
        xr = sb("xr", [P, QT, C], F32)
        y32 = sb("y32", [P, QT, C], F32)
        yhl = sb("yhl", [P, 2, QT, C], F16)
        yt = sb("yt", [P, 2, CC, QB], F16)
        st = sb("st", [P, QT, 6], F32)
        mv = sb("mv", [P, QT, 2], F32)
        ve = sb("ve", [P, QT], F32)
        rstd = sb("rstd", [P, QT], F32)
        mhalf = sb("mhalf", [P, QT], F32)
        p32 = sb("p32", [P, 2, 2, QB], F32)
        phi = sb("phi", [P, 4, 2, QB], F16)
        plo = sb("plo", [P, 4, 2, QB], F16)
        mpart = sb("mpart", [P, QT, 8], F32)
        mrow = sb("mrow", [P, QT], F32)
        negm = sb("negm", [P, QT], F16)
        oe = sb("oe", [P, QT, C + 1], F32)
        rz = sb("rz", [P, QT], F32)
        tb = sb("tb", [P, QT, C], F32)
        est = sb("est", [P, QT, 6], F32)
        emv = sb("emv", [P, QT, 2], F32)
        eve = sb("eve", [P, QT], F32)
        erstd = sb("erstd", [P, QT], F32)
        wdot = sb("wdot", [P, QT], F32)
        wjunk = sb("wjunk", [P, QT, C], F32)
        lnb = sb("lnb", [P, QT, C], F32)
        res = sb("res", [P, QT, C], F32)
        wcol = sb("wcol", [P, NT], F32)
        wsel = sb("wsel", [P, NT], F32)
        pk = sb("pk", [P, NT, 2], F32)
        tok = sb("tok", [P, NT], I32)
        tokf = sb("tokf", [P, NT], F32)
        rbase = sb("rbase", [P, 1], F32)
        cand_i = sb("cand_i", [P, 15], I32)
        cand1 = sb("cand1", [P, 15], F32)
        keym = sb("keym", [P, NT], I32)
        key = sb("key", [P, NT], I32)
        kpart = sb("kpart", [P, NT], I32)
        khi = sb("khi", [P, NT], F32)
        klo = sb("klo", [P, NT], F32)
        val = sb("val", [P, NT], F32)
        vtmp = sb("vtmp", [P, NT], F32)
        base = sb("base", [P, 2], F32)
        cand = sb("cand", [P, 15], F32)
        cmp = sb("cmp", [P, 15, NT], F32)
        cnt = sb("cnt", [P, 15], F16)
        isge = sb("isge", [P, 15], F32)
        nge = sb("nge", [P, 1], F32)
        gt16 = sb("gt16", [P, NT], F16)
        eq16 = sb("eq16", [P, NT], F16)
        sel16 = sb("sel16", [P, NT], F16)
        csum = sb("csum", [P, NT], F32)
        cexc = sb("cexc", [P, NT], F32)
        zeros = sb("zeros", [P, NT], F32)
        rank = sb("rank", [P, NT], F32)
        need = sb("need", [P, 1], F32)
        ngt = sb("ngt", [P, 1], F32)
        take = sb("take", [P, NT], F32)
        drop = sb("drop", [P, NT], F32)
        rowf = sb("rowf", [P, NT], F32)
        rowi = sb("rowi", [P, NT], I32)
        rowb = sb("rowb", [P, 2, FT, C], F32)
        idw = sb("idw", [P, RING, FT, 2], F32)
        thl = sb("thl", [P, 2, FT, C], F16)
        tt = sb("tt", [P, 2, 2, CC, FB], F16)
        h32, hhi, hlo = p32, phi, plo
        yb = tb
        zb = sb("zb", [P, 2, FT, C], F32)

        stage = vs[1][:, :, :].rearrange("p a b -> p (a b)").bitcast(F32)
        sizes = [CC * P, CC * P, CC * C, CC * HID, HC * C]
        starts = [sum(sizes[:i]) for i in range(len(sizes))]
        staged = [stage[:, a:a + n] for a, n in zip(starts, sizes)]
        split = [w[:, :, :, :].rearrange("p h a b -> p h (a b)") for w in (wq_s, wk_s, wv_s, w1_s, w2_s)]

        bank = [ctx.enter_context(nc.psum_tensor(f"bank{i}", [P, 512], F32)) for i in range(8)]
        s_bank = [bank[0], bank[1]]
        m_bank = [bank[2], bank[3]]
        o_bank = [bank[4], bank[5]]
        r_bank = bank[6]
        p_bank = bank[7]
        h_bank = [bank[0], bank[1]]
        y_bank = [bank[2], bank[3]]
        x_bank = bank[4]

        def f16(b):
            return b[:, :].bitcast(F16)

        weights_in = sem("weights_in")
        xp_in = sem("xp_in")
        xr_in = sem("xr_in")
        consts = sem("consts")
        waits_settled = sem("waits_settled")
        consts_dve = sem("consts_dve")
        w_hi = sem("w_hi")
        w_lo = sem("w_lo")
        var_ready = sem("var_ready")
        dve_p = sem("dve_p")
        rstd_ready = sem("rstd_ready")
        y_ready = sem("y_ready")
        yhi_ready = sem("yhi_ready")
        ylo_ready = sem("ylo_ready")
        t_done = sem("t_done")
        yt_ready = sem("yt_ready")
        kq_done = sem("kq_done")
        kqhi_ready = sem("kqhi_ready")
        kqlo_ready = sem("kqlo_ready")
        v_done = sem("v_done")
        vhi_ready = sem("vhi_ready")
        vlo_ready = sem("vlo_ready")
        s_done = sem("s_done")
        exp_done = sem("exp_done")
        hi_done = sem("hi_done")
        lo_done = sem("lo_done")
        pv_done = sem("pv_done")
        m_done = sem("m_done")
        m_read = sem("m_read")
        dve_m = sem("dve_m")
        negm_ready = sem("negm_ready")
        row_done = sem("row_done")
        row_ready = sem("row_ready")
        xr_ready = sem("xr_ready")
        o_read = sem("o_read")
        dve_e = sem("dve_e")
        evar_ready = sem("evar_ready")
        erstd_ready = sem("erstd_ready")
        ln_ready = sem("ln_ready")
        ln_out = sem("ln_out")
        w_ready = sem("w_ready")
        res_ready = sem("res_ready")
        res_out = sem("res_out")
        dve_r = sem("dve_r")
        cnt_ready = sem("cnt_ready")
        tot_ready = sem("tot_ready")
        rows_ready = sem("rows_ready")
        pack_out = sem("pack_out")
        id_in = [sem(f"id_in{i}") for i in range(RING)]
        f_in = [sem(f"f_in{i}") for i in range(RING)]
        thi_ready = sem("thi_ready")
        tlo_ready = sem("tlo_ready")
        ft_done = sem("ft_done")
        tt_ready = sem("tt_ready")
        h_done = sem("h_done")
        gelu_done = sem("gelu_done")
        hhi_ready = sem("hhi_ready")
        hlo_ready = sem("hlo_ready")
        w2_done = sem("w2_done")
        y_read = sem("y_read")
        z_ready = sem("z_ready")
        z_out = [sem(f"z_out{i}") for i in range(RING)]

        E_N = 9
        P_N = 2 * QT
        own_order = [0]
        ROUTE_PARTS = 11
        ROUTE_AT = {0: 0, 2: 1, 4: 2, 6: 3, 8: 4, 10: 5}
        RC_N = 10

        WEIGHTS = 14 * 16
        CONSTS_DVE = 10

        def settled(eng):
            eng.sem_inc(waits_settled, 1)

        block = ctx.enter_context(nc.Block())

        @block.sync
        def _(sp):
            for k, w in enumerate((wq, wk, wv, w1, w2)):
                sp.dma_start(staged[k], w).then_inc(weights_in, 16)
            for s, w in ((bq_s, bq), (bk_s, bk), (br_s, br), (b1_s, b1), (wr_s, wr)):
                sp.dma_start(s[:, :], w).then_inc(weights_in, 16)
            for s, w in ((bv_s, bv), (b2_s, b2)):
                for i in range(2):
                    sp.dma_start(s[:, i, :], w).then_inc(weights_in, 16)

            def of_block(view, k):
                return view[bass.ds(k, 1)].rearrange("k p t c -> p (k t) c")

            def load_projected(h):
                sp.wait_ge(y_ready, h * QT + QT)
                sp.dma_start(xp[:, :, :], of_block(x_v, h)).then_inc(xp_in, 16)

            def load_residual(k):
                sp.wait_ge(dve_e, k * E_N + 3)
                sp.dma_start(xr[:, :, :], of_block(x_v, k)).then_inc(xr_in, 16)

            def store_ln(k):
                sp.wait_ge(ln_ready, k * QT + QT)
                sp.dma_start(of_block(ln_v, k), lnb[:, :, :]).then_inc(ln_out, 16)

            def store_sum(k):
                sp.wait_ge(res_ready, k + 2)
                sp.dma_start(of_block(out_v, k), res[:, :, :]).then_inc(res_out, 16)

            with sp.Fori(0, AHEAD + 1) as h:
                load_projected(h)
            load_residual(0)
            load_projected(AHEAD + 1)
            with sp.Fori(1, BLOCKS - AHEAD - 1) as k:
                load_residual(k)
                load_projected(k + AHEAD + 1)
                store_ln(k - 1)
                store_sum(k - 1)
            with sp.Fori(BLOCKS - AHEAD - 1, BLOCKS) as k:
                load_residual(k)
                store_ln(k - 1)
                store_sum(k - 1)
            store_ln(BLOCKS - 1)
            store_sum(BLOCKS - 1)

            sp.wait_ge(pack_out, (B - 1) * NT * 16)

            def load_ids(f, ring):
                sp.dma_start(idw[:, ring, :, :],
                             packed_v[bass.ds(f, 1)].rearrange("f p t c -> p (f t) c")).then_inc(id_in[ring], 16)

            def load_ids_of(i):
                for ring in range(RING):
                    sp.wait_ge(z_out[ring], i * (FT * 16))
                    load_ids(i * RING + ring, ring)

            for ring in range(RING):
                load_ids(ring, ring)
            with sp.Fori(1, NI - NI // B) as i:
                load_ids_of(i)
            sp.wait_ge(pack_out, B * NT * 16)
            with sp.Fori(NI - NI // B, NI) as i:
                load_ids_of(i)
            sp.wait_ge(ln_out, BLOCKS * 16 + 16)
            sp.wait_ge(res_out, BLOCKS * 16 + 16)
            for ring in range(RING):
                sp.wait_ge(z_out[ring], NI * FT * 16)

        @block.gpsimd
        def _(pool):
            G = nc.gpsimd
            G.memset(ident[:, :], 0.0).then_inc(consts, 1)
            G.memset(tri16[:, :], 0.0).then_inc(consts, 1)
            G.iota(tok[:, :], pattern=[[P, NT]], base=0, channel_multiplier=1).then_inc(consts, 1)
            G.iota(cand_i[:, :], pattern=[[1, 15]], base=1, channel_multiplier=0).then_inc(consts, 1)
            pool.wait_ge(consts, 4)
            G.affine_select(out=ident[:, :], in_=ident[:, :], compare_op=ALU.not_equal, fill=1.0,
                            base=0, pattern=[[-1, P]], channel_multiplier=1).then_inc(consts, 1)
            G.affine_select(out=tri16[:, :], in_=tri16[:, :], compare_op=ALU.is_ge, fill=1.0,
                            base=0, pattern=[[-1, P]], channel_multiplier=1).then_inc(consts, 1)

            def project_rstd(h):
                pool.wait_ge(var_ready, h + 1)
                G.tensor_tensor(rstd[:, :], ve[:, :], mhalf[:, :], ALU.pow).then_inc(rstd_ready, 1)

            def project_lo(h):
                pool.wait_ge(yhi_ready, h + 1)
                pool.wait_ge(t_done, h + 1)
                G.tensor_tensor(yhl[:, 1, :, :], y32[:, :, :], yhl[:, 0, :, :], ALU.subtract).then_inc(ylo_ready, 1)

            def end_rstd(k):
                pool.wait_ge(evar_ready, k + 1)
                G.tensor_tensor(erstd[:, :], eve[:, :], mhalf[:, :], ALU.pow).then_inc(erstd_ready, 1)

            def residual(k):
                pool.wait_ge(xr_in, k * 16 + 16)
                G.tensor_tensor(xr[:, :, :], xr[:, :, :], bv_s[:, :, :], ALU.add).then_inc(xr_ready, 1)

            def end_sum(k):
                pool.wait_ge(ln_ready, k * QT + QT)
                pool.wait_ge(res_out, k * 16 + 16)
                G.tensor_tensor(res[:, :, :], tb[:, :, :], lnb[:, :, :], ALU.add).then_inc(res_ready, 1)

            def pack(tiles):
                for t in tiles:
                    G.indirect_dma_start(
                        out=packed, out_offset=bass.IndirectOffsetOnAxis(ap=rowi[:, t:t + 1].bitcast(U32), axis=0),
                        in_=pk[:, t, :], in_offset=None, bounds_check=ROWS - 1, oob_is_err=False,
                    ).then_inc(pack_out, 16)

            def attend(k, first, projects):
                if projects:
                    project_rstd(k + AHEAD)
                if not first:
                    end_rstd(k - 1)
                residual(k)
                if projects:
                    project_lo(k + AHEAD)
                if not first:
                    end_sum(k - 1)

            pool.wait_ge(weights_in, WEIGHTS)
            pool.wait_ge(consts_dve, CONSTS_DVE)
            project_rstd(0)
            project_lo(0)
            with pool.Fori(1, AHEAD) as h:
                project_rstd(h)
                project_lo(h)
            attend(0, True, True)
            with pool.Fori(1, NB) as k:
                attend(k, False, True)
            for b in range(1, B):
                for nb in range(3):
                    attend(b * NB + nb, False, b < B - 1)
                pool.wait_ge(rows_ready, b)
                for nb in range(3, 11):
                    pack(range((nb - 3) * 4, (nb - 2) * 4))
                    attend(b * NB + nb, False, b < B - 1)
                pool.wait_ge(pack_out, b * NT * 16)
                with pool.Fori(11, NB - 1) as nb:
                    attend(b * NB + nb, False, b < B - 1)
                attend(b * NB + NB - 1, False, b < B - 2)
            end_rstd(BLOCKS - 1)
            end_sum(BLOCKS - 1)

            def gather(f, i, ring):
                pool.wait_ge(id_in[ring], i * 16 + 16)
                if not (isinstance(f, int) and f < 2):
                    pool.wait_ge(tlo_ready, f - 1)
                    settled(pool)
                for t in range(FT):
                    G.indirect_dma_start(
                        out=rowb[:, ring % 2, t, :], out_offset=None, in_=ln_rows,
                        in_offset=bass.IndirectOffsetOnAxis(ap=idw[:, ring, t, 1:2].bitcast(U32), axis=0),
                        bounds_check=B * N - 1,
                    ).then_inc(f_in[ring], 16)

            def scatter(f, ring):
                pool.wait_ge(z_ready, f * FT + FT)
                settled(pool)
                for t in range(FT):
                    G.indirect_dma_start(
                        out=out,
                        out_offset=bass.IndirectOffsetOnAxis(ap=idw[:, ring, t, 1:2].bitcast(U32), axis=0),
                        in_=zb[:, ring % 2, t, :], in_offset=None, bounds_check=B * N - 1, compute_op=ALU.add,
                    ).then_inc(z_out[ring], 16)

            pool.wait_ge(ln_out, BLOCKS * 16 + 16)
            pool.wait_ge(res_out, BLOCKS * 16 + 16)

            def mlp(i, packs, last):
                for ring in range(RING):
                    if not (last and ring >= RING - 2):
                        gather(i * RING + ring + 2, i + (ring + 2) // RING, (ring + 2) % RING)
                    if packs is not None:
                        pack(range(packs + ring * 2, packs + ring * 2 + 2))
                    scatter(i * RING + ring, ring)

            gather(0, 0, 0)
            gather(1, 0, 1)
            mlp(0, None, False)
            pool.wait_ge(rows_ready, B)
            for i in range(1, 5):
                mlp(i, (i - 1) * 8, False)
            with pool.Fori(5, NI - 1) as i:
                mlp(i, None, False)
            mlp(NI - 1, None, True)

        @block.scalar
        def _(act):
            A = nc.scalar
            act.wait_ge(weights_in, WEIGHTS)
            for s, w in zip(staged, split):
                A.copy(w[:, 0, :], s).then_inc(w_hi, 1)

            def y_hi(h):
                act.wait_ge(y_ready, h * QT + QT + 2)
                act.wait_ge(t_done, h + 1)
                A.copy(yhl[:, 0, :, :], y32[:, :, :]).then_inc(yhi_ready, 1)

            def y_t(h):
                act.wait_ge(t_done, h + 2)
                A.copy(yt[:, :, :, :].rearrange("p h c n -> p (h c n)"), f16(p_bank)).then_inc(yt_ready, 1)

            def kq_hi(h, par, nb):
                cols = bass.ds(nb * QB, QB)
                act.wait_ge(kq_done, h + 1)
                A.activation(ka[par][:, cols], p_bank[:, 0:QB], ACT.Identity, bias=bk_s[:, 0:1])
                A.activation(qb[par][:, cols], p_bank[:, QB:2 * QB], ACT.Identity, bias=bq_s[:, 0:1])
                A.activation(qa[par][0:D, cols], p_bank[0:D, QB:2 * QB], ACT.Identity, bias=bq_s[0:D, 0:1]
                             ).then_inc(kqhi_ready, 1)

            def v_hi(h, par, nb):
                act.wait_ge(v_done, h + 1)
                A.copy(vs[par][:, bass.ds(nb * QT, QT), 0:C], p_bank[:, :].rearrange("p (t c) -> p t c", t=QT)
                       ).then_inc(vhi_ready, 1)

            def exponent(t, j):
                act.wait_ge(s_done, t + 1)
                act.wait_ge(lo_done, t + 1)
                A.activation(p32[:, j % 2, :, :].rearrange("p m n -> p (m n)"), s_bank[j % 2][:, :], ACT.Exp
                             ).then_inc(exp_done, 1)

            def p_hi(t, j):
                act.wait_ge(exp_done, t + 3)
                act.wait_ge(pv_done, t + 1)
                A.copy(phi[:, j % 4, :, :], p32[:, j % 2, :, :]).then_inc(hi_done, 1)

            def evacuate(k):
                act.wait_ge(pv_done, k * STEPS + STEPS + 4)
                for i in range(QT):
                    last = A.copy(oe[:, i, :], o_bank[i][:, 0:C + 1])
                last.then_inc(o_read, 1)

            def row(k, par, nb):
                act.wait_ge(row_done, k + 1)
                A.copy(qb[par][D:D + 1, bass.ds(nb * QB, QB)], r_bank[D:D + 1, 0:QB]).then_inc(row_ready, 1)

            def attend(k, following, projected, first=False):
                for j in range(STEPS):
                    t = k * STEPS + j
                    p_hi(t, j)
                    if j + 1 < STEPS or following:
                        exponent(t + 1, (j + 1) % STEPS)
                    if j == 0 and not first:
                        evacuate(k - 1)
                    if j == 13 and following:
                        row(k + 1, *following)
                    if projected:
                        if j == 5:
                            y_hi(k + AHEAD)
                        elif j == 9:
                            y_t(k + AHEAD)
                        elif j == 11:
                            kq_hi(k + AHEAD, *projected)
                        elif j == 14:
                            v_hi(k + AHEAD, *projected)

            y_hi(0)
            y_t(0)
            with act.Fori(0, NB) as h:
                y_hi(h + 1)
                kq_hi(h, 0, h)
                v_hi(h, 0, h)
                y_t(h + 1)
            kq_hi(NB, 1, 0)
            v_hi(NB, 1, 0)
            row(0, 0, 0)
            exponent(0, 0)
            for b in range(B):
                par, k0 = b % 2, b * NB
                if b == 0:
                    attend(0, (par, 1), (1 - par, 1), first=True)
                with act.Fori(b == 0, NB - 1) as nb:
                    attend(k0 + nb, (par, nb + 1), (1 - par, nb + 1) if b < B - 1 else None)
                attend(k0 + NB - 1, (1 - par, 0) if b < B - 1 else None, (par, 0) if b < B - 2 else None)
            evacuate(BLOCKS - 1)

            def row_hi(f, ring, i):
                act.wait_ge(f_in[ring], (i + 1) * (FT * 16))
                act.wait_ge(ft_done, f + 1)
                A.copy(thl[:, 0, :, :], rowb[:, ring % 2, :, :]).then_inc(thi_ready, 1)

            def mlp(f, ring, i, last):
                for p in range(HC // 2):
                    q = f * (HC // 2) + p
                    act.wait_ge(h_done, q + 1)
                    act.wait_ge(hlo_ready, q + 1)
                    A.activation(h32[:, p % 2, 0, :], h_bank[p % 2][:, 0:FB], ACT.Gelu_apprx_tanh,
                                 bias=b1_s[:, 2 * p:2 * p + 1])
                    A.activation(h32[:, p % 2, 1, :], h_bank[p % 2][:, FB:2 * FB], ACT.Gelu_apprx_tanh,
                                 bias=b1_s[:, 2 * p + 1:2 * p + 2]).then_inc(gelu_done, 1)
                    act.wait_ge(gelu_done, q + 3)
                    act.wait_ge(w2_done, q + 1)
                    A.copy(hhi[:, p % 2, :, :], h32[:, p % 2, :, :]).then_inc(hhi_ready, 1)
                    if p == 0 and not last:
                        row_hi(f + 1, (ring + 1) % RING, i + (ring + 1) // RING)

            row_hi(0, 0, 0)
            with act.Fori(0, NI - 1) as i:
                for ring in range(RING):
                    mlp(i * RING + ring, ring, i, False)
            for ring in range(RING):
                mlp(NF - RING + ring, ring, NI - 1, ring == RING - 1)

        @block.vector
        def _(dve):
            V = nc.vector
            for s, n in ((y_ready, 2), (ylo_ready, 1), (t_done, 1), (vlo_ready, 1), (exp_done, 2), (lo_done, 2),
                         (pv_done, 4), (m_read, 2), (o_read, 1), (dve_e, E_N), (res_ready, 1), (ln_out, 16),
                         (res_out, 16), (ft_done, 1), (tt_ready, 1), (gelu_done, 2), (hlo_ready, 2), (w2_done, 2),
                         (y_read, 2)):
                dve.sem_inc(s, n)
            V.memset(ones16[:, :], 1.0).then_inc(consts_dve, 1)
            V.memset(mhalf[:, :], -0.5).then_inc(consts_dve, 1)
            V.memset(zeros[:, :], 0.0).then_inc(consts_dve, 1)
            V.memset(rbase[:, :], 0.0).then_inc(consts_dve, 1)
            dve.wait_ge(consts, 6)
            V.tensor_copy(cand1[:, :], cand_i[:, :]).then_inc(consts_dve, 1)
            V.tensor_copy(tokf[:, :], tok[:, :]).then_inc(consts_dve, 1)
            for n, (s, w) in enumerate(zip(staged, split)):
                dve.wait_ge(w_hi, n + 1)
                V.tensor_tensor(w[:, 1, :], s, w[:, 0, :], ALU.subtract).then_inc(w_lo, 1)
            dve.wait_ge(w_lo, 5)
            for i in range(2):
                V.memset(vs[i][:, :, C:C + 1], 1.0).then_inc(consts_dve, 1)
                V.memset(kb[i][D:D + 1, :], 1.0).then_inc(consts_dve, 1)

            def variance(h):
                dve.wait_ge(xp_in, h * 16 + 16)
                for t in range(QT):
                    V.bn_stats(st[:, t, :], xp[:, t, :]).then_inc(dve_p, 1)

            def var_eps(h):
                dve.wait_ge(dve_p, h * P_N + QT)
                settled(dve)
                for t in range(QT):
                    V.bn_aggr(mv[:, t, :], st[:, t, :]).then_inc(dve_p, 1)
                dve.wait_ge(dve_p, h * P_N + 2 * QT)
                V.tensor_scalar(ve[:, :], mv[:, :, 1], 1e-6, None, ALU.add).then_inc(var_ready, 1)

            def normalise(h):
                dve.wait_ge(rstd_ready, h + 1)
                dve.wait_ge(ylo_ready, h + 1)
                for t in range(QT):
                    V.tensor_scalar(y32[:, t, :], xp[:, t, :], mv[:, t, 0:1], rstd[:, t:t + 1],
                                    ALU.subtract, ALU.mult).then_inc(y_ready, 1)

            def kq_lo(h, par, nb):
                cols = bass.ds(nb * QB, QB)
                dve.wait_ge(kqhi_ready, h + 1)
                V.scalar_tensor_tensor(out=kb[par][0:D, cols], in0=p_bank[0:D, 0:QB], scalar=bk_s[0:D, 0:1],
                                       in1=ka[par][0:D, cols], op0=ALU.add, op1=ALU.subtract)
                V.scalar_tensor_tensor(out=qa[par][D:2 * D, cols], in0=p_bank[D:2 * D, QB:2 * QB],
                                       scalar=bq_s[D:2 * D, 0:1], in1=qb[par][D:2 * D, cols],
                                       op0=ALU.add, op1=ALU.subtract).then_inc(kqlo_ready, 1)

            def v_lo(h, par, nb):
                dve.wait_ge(vhi_ready, h + 1)
                tiles = bass.ds(nb * QT, QT)
                V.tensor_tensor(vs[par][:, tiles, VLO:VLO + C], p_bank[:, :].rearrange("p (t c) -> p t c", t=QT),
                                vs[par][:, tiles, 0:C], ALU.subtract).then_inc(vlo_ready, 1)

            def p_lo(t, j):
                dve.wait_ge(hi_done, t + 1)
                V.tensor_tensor(plo[:, j % 4, :, :], p32[:, j % 2, :, :], phi[:, j % 4, :, :],
                                ALU.subtract).then_inc(lo_done, 1)

            def unit_max(k, u):
                dve.wait_ge(m_done, k * UNITS + u + 1)
                V.tensor_reduce(mpart[:, u // 8, u % 8:u % 8 + 1], m_bank[u % 2][:, :], AX.X, ALU.max
                                ).then_inc(m_read, 1)

            def row_max(k):
                dve.wait_ge(m_read, k * UNITS + UNITS + 2)
                V.tensor_reduce(mrow[:, :], mpart[:, :, :], AX.X, ALU.max).then_inc(dve_m, 1)
                dve.wait_ge(dve_m, k + 1)
                V.tensor_scalar(negm[:, :], mrow[:, :], -1.0, SHIFT, ALU.mult, ALU.add).then_inc(negm_ready, 1)

            def end_block(k, nb, part):
                e0 = k * E_N + E_N
                if part == 0:
                    dve.wait_ge(o_read, k + 2)
                    V.reciprocal(rz[:, :], oe[:, :, C]).then_inc(dve_e, 1)
                elif part == 1:
                    dve.wait_ge(dve_e, e0 + 1)
                    dve.wait_ge(xr_ready, k + 1)
                    dve.wait_ge(res_ready, k + 1)
                    for i in range(QT):
                        V.scalar_tensor_tensor(out=tb[:, i, :], in0=oe[:, i, 0:C], scalar=rz[:, i:i + 1],
                                               in1=xr[:, i, :], op0=ALU.mult, op1=ALU.add).then_inc(dve_e, 1)
                elif part == 2:
                    dve.wait_ge(dve_e, e0 + 3)
                    for i in range(QT):
                        V.bn_stats(est[:, i, :], tb[:, i, :]).then_inc(dve_e, 1)
                elif part == 3:
                    dve.wait_ge(dve_e, e0 + 5)
                    settled(dve)
                    for i in range(QT):
                        V.bn_aggr(emv[:, i, :], est[:, i, :]).then_inc(dve_e, 1)
                    dve.wait_ge(dve_e, e0 + 7)
                    V.tensor_scalar(eve[:, :], emv[:, :, 1], 1e-5, None, ALU.add).then_inc(evar_ready, 1)
                elif part == 4:
                    dve.wait_ge(erstd_ready, k + 1)
                    dve.wait_ge(ln_out, k * 16 + 16)
                    for i in range(QT):
                        V.tensor_scalar(lnb[:, i, :], tb[:, i, :], emv[:, i, 0:1], erstd[:, i:i + 1],
                                        ALU.subtract, ALU.mult).then_inc(ln_ready, 1)
                elif part == 5:
                    dve.wait_ge(ln_ready, k * QT + QT)
                    for i in range(QT):
                        V.tensor_tensor_reduce(out=wjunk[:, i, :], in0=lnb[:, i, :], in1=wr_s[:, :], scale=1.0,
                                               scalar=0.0, op0=ALU.mult, op1=ALU.add, accum_out=wdot[:, i:i + 1]
                                               ).then_inc(dve_e, 1)
                elif part == 6:
                    dve.wait_ge(dve_e, e0 + 9)
                    V.tensor_scalar(wcol[:, bass.ds(nb * QT, QT)], wdot[:, :], br_s[:, 0:1], None, ALU.add
                                    ).then_inc(w_ready, 1)

            PART_AT = {1: 0, 2: 1, 4: 2, 5: 3, 6: 4, 7: 5, 8: 6}

            def attend(k, following, projected, ended, routed=None):
                u = 0
                for j in range(STEPS):
                    p_lo(k * STEPS + j, j)
                    if following:
                        for _ in range(UNIT_OF[j]):
                            unit_max(k + 1, u)
                            u += 1
                        if UNIT_OF[j] and u == UNITS:
                            row_max(k + 1)
                    if j in PART_AT and ended is not None:
                        end_block(k - 1, ended, PART_AT[j])
                    if projected:
                        if j == 0:
                            variance(k + AHEAD)
                        elif j == 3:
                            var_eps(k + AHEAD)
                        elif j == 4:
                            normalise(k + AHEAD)
                        elif j == 12:
                            kq_lo(k + AHEAD, *projected)
                        elif j == 15:
                            v_lo(k + AHEAD, *projected)
                    if routed and j in ROUTE_AT and routed[1] + ROUTE_AT[j] < ROUTE_PARTS:
                        route(routed[0], routed[1] + ROUTE_AT[j])

            def route(b, part):

                def own(ins):
                    ins.then_inc(dve_r, 1)
                    own_order[0] += 1
                    dve.wait_ge(dve_r, own_order[0])

                def count(vals, col, step):
                    own(V.tensor_scalar(cand[:, :], cand1[:, :], step, base[:, col:col + 1], ALU.mult, ALU.add))
                    own(V.tensor_tensor(cmp[:, :, :], vals[:, :].unsqueeze(1).to_broadcast([P, 15, NT]),
                                        cand[:, :].unsqueeze(2).to_broadcast([P, 15, NT]), ALU.is_ge))
                    with nc.allow_low_precision(reason="counts up to 32 are exact"):
                        V.tensor_reduce(cnt[:, :], cmp[:, :, :], AX.X, ALU.add).then_inc(cnt_ready, 1)

                def advance(col, step):
                    own(V.tensor_scalar(isge[:, :], sums[:, 0:15], KEEP - 0.5, None, ALU.is_ge))
                    own(V.tensor_reduce(nge[:, :], isge[:, :], AX.X, ALU.add))
                    own(V.scalar_tensor_tensor(out=base[:, col:col + 1], in0=nge[:, :], scalar=step,
                                               in1=base[:, col:col + 1], op0=ALU.mult, op1=ALU.add))

                def rank_of(col_sums, prefix):
                    own(V.tensor_tensor_scan(csum[:, :], zeros[:, :], col_sums, 0.0, ALU.add, ALU.add))
                    own(V.tensor_tensor(cexc[:, :], csum[:, :], col_sums, ALU.subtract))
                    own(V.tensor_tensor(rank[:, :], cexc[:, :], prefix, ALU.add))

                sums = r_bank[:, QB:QB + 3 * NT]
                steps = (4096.0, 256.0, 16.0, 1.0)
                if part > 0:
                    dve.wait_ge(tot_ready, b * RC_N + part)
                if part == 0:
                    dve.wait_ge(w_ready, (b + 1) * NB)
                    own(V.tensor_copy(wsel[:, :], wcol[:, :]))
                    w_i = wsel[:, :].bitcast(I32)
                    own(V.tensor_scalar(keym[:, :], w_i, 31, -2147483648, ALU.arith_shift_right, ALU.bitwise_or))
                    own(V.tensor_tensor(key[:, :], w_i, keym[:, :], ALU.bitwise_xor))
                    own(V.tensor_scalar(kpart[:, :].bitcast(U32), key[:, :].bitcast(U32), 16, None,
                                        ALU.logical_shift_right))
                    own(V.tensor_copy(khi[:, :], kpart[:, :]))
                    own(V.tensor_scalar(kpart[:, :], key[:, :], 65535, None, ALU.bitwise_and))
                    own(V.tensor_copy(klo[:, :], kpart[:, :]))
                    own(V.memset(base[:, :], 0.0))
                    count(khi, 0, steps[0])
                elif part < 4:
                    advance(0, steps[part - 1])
                    count(khi, 0, steps[part])
                elif part == 4:
                    advance(0, steps[3])
                    own(V.tensor_scalar(vtmp[:, :], klo[:, :], 1.0, None, ALU.add))
                    own(V.scalar_tensor_tensor(out=vtmp[:, :], in0=khi[:, :], scalar=base[:, 0:1], in1=vtmp[:, :],
                                               op0=ALU.is_equal, op1=ALU.mult))
                    own(V.tensor_scalar(val[:, :], khi[:, :], base[:, 0:1], 70000.0, ALU.is_gt, ALU.mult))
                    own(V.scalar_tensor_tensor(out=val[:, :], in0=val[:, :], scalar=-1.0, in1=vtmp[:, :],
                                               op0=ALU.add, op1=ALU.add))
                    count(val, 1, steps[0])
                elif part < 8:
                    advance(1, steps[part - 5])
                    count(val, 1, steps[part - 4])
                elif part == 8:
                    advance(1, steps[3])
                    own(V.tensor_scalar(gt16[:, :], val[:, :], base[:, 1:2], None, ALU.is_gt))
                    V.tensor_scalar(eq16[:, :], val[:, :], base[:, 1:2], None, ALU.is_equal).then_inc(cnt_ready, 1)
                elif part == 9:
                    own(V.tensor_reduce(ngt[:, :], sums[:, 0:NT], AX.X, ALU.add))
                    own(V.tensor_scalar(need[:, :], ngt[:, :], -1.0, float(KEEP), ALU.mult, ALU.add))
                    rank_of(sums[:, NT:2 * NT], sums[:, 2 * NT:3 * NT])
                    own(V.scalar_tensor_tensor(out=take[:, :], in0=rank[:, :], scalar=need[:, 0:1], in1=eq16[:, :],
                                               op0=ALU.is_lt, op1=ALU.mult))
                    V.tensor_tensor(sel16[:, :], take[:, :], gt16[:, :], ALU.add).then_inc(cnt_ready, 1)
                    own(V.tensor_scalar(drop[:, :], rank[:, :], 1.0, need[:, 0:1], ALU.add, ALU.is_equal))
                    own(V.tensor_tensor(drop[:, :], drop[:, :], eq16[:, :], ALU.mult))
                    own(V.tensor_scalar(drop[:, :], drop[:, :], -1.0, 1.0, ALU.mult, ALU.add))
                    own(V.tensor_tensor(pk[:, :, 0], wsel[:, :], drop[:, :], ALU.mult))
                    own(V.tensor_copy(pk[:, :, 1].bitcast(I32), tokf[:, :]))
                    own(V.tensor_scalar(tokf[:, :], tokf[:, :], float(N), None, ALU.add))
                else:
                    rank_of(sums[:, 0:NT], sums[:, NT:2 * NT])
                    own(V.scalar_tensor_tensor(out=rowf[:, :], in0=rank[:, :], scalar=rbase[:, 0:1], in1=sel16[:, :],
                                               op0=ALU.add, op1=ALU.mult))
                    own(V.tensor_scalar(take[:, :], sel16[:, :], -BIG, BIG, ALU.mult, ALU.add))
                    own(V.tensor_tensor(rowf[:, :], rowf[:, :], take[:, :], ALU.add))
                    own(V.tensor_scalar(rbase[:, :], rbase[:, :], float(KEEP), None, ALU.add))
                    V.tensor_copy(rowi[:, :], rowf[:, :]).then_inc(rows_ready, 1)

            variance(0)
            var_eps(0)
            normalise(0)
            with dve.Fori(0, NB) as h:
                variance(h + 1)
                var_eps(h + 1)
                normalise(h + 1)
                kq_lo(h, 0, h)
                v_lo(h, 0, h)
            kq_lo(NB, 1, 0)
            v_lo(NB, 1, 0)
            for u in range(UNITS):
                unit_max(0, u)
            row_max(0)
            for b in range(B):
                par, k0 = b % 2, b * NB
                projects, begin = b < B - 1, 1
                if b == 0:
                    attend(0, (par, 1), (1 - par, 1), None)
                else:
                    attend(k0, (par, 1), (1 - par, 1) if projects else None, NB - 1)
                    for nb, part in ((1, 0), (2, len(ROUTE_AT))):
                        attend(k0 + nb, (par, nb + 1), (1 - par, nb + 1) if projects else None, nb - 1, (b - 1, part))
                    begin = 3
                with dve.Fori(begin, NB - 1) as nb:
                    attend(k0 + nb, (par, nb + 1), (1 - par, nb + 1) if projects else None, nb - 1)
                attend(k0 + NB - 1, (1 - par, 0) if projects else None, (par, 0) if b < B - 2 else None, NB - 2)
            for part in range(7):
                end_block(BLOCKS - 1, NB - 1, part)

            dve.wait_ge(res_ready, BLOCKS + 1)

            def row_lo(f, ring):
                dve.wait_ge(thi_ready, f + 1)
                V.tensor_tensor(thl[:, 1, :, :], rowb[:, ring % 2, :, :], thl[:, 0, :, :], ALU.subtract
                                ).then_inc(tlo_ready, 1)

            def rows_t(f, ring):
                dve.wait_ge(ft_done, f + 2)
                V.tensor_copy(tt[:, ring % 2, :, :, :].rearrange("p h c n -> p (h c n)"), f16(x_bank)
                              ).then_inc(tt_ready, 1)

            def finish(f, ring, i):
                dve.wait_ge(w2_done, f * 4 + 6)
                V.tensor_tensor(yb[:, :, :], y_bank[ring % 2][:, :].rearrange("p (t c) -> p t c", t=FT), b2_s[:, :, :],
                                ALU.add).then_inc(y_read, 1)
                dve.wait_ge(y_read, f + 3)
                if ring >= 2:
                    dve.wait_ge(z_out[ring - 2], (i + 1) * (FT * 16))
                elif not isinstance(i, int) or i > 0:
                    dve.wait_ge(z_out[ring + 2], i * (FT * 16))
                for t in range(FT):
                    V.tensor_scalar(zb[:, ring % 2, t, :], yb[:, t, :], idw[:, ring, t, 0:1], None, ALU.mult
                                    ).then_inc(z_ready, 1)

            def mlp(f, ring, i, first, last, part=None):
                for p in range(HC // 2):
                    dve.wait_ge(hhi_ready, f * 4 + p + 1)
                    V.tensor_tensor(hlo[:, p % 2, :, :], h32[:, p % 2, :, :], hhi[:, p % 2, :, :], ALU.subtract
                                    ).then_inc(hlo_ready, 1)
                    if p == 0 and not last:
                        row_lo(f + 1, (ring + 1) % RING)
                    if p == 1 and not first:
                        finish(f - 1, (ring - 1) % RING, i if ring else i - 1)
                    if p == 2 and not last:
                        rows_t(f + 1, (ring + 1) % RING)
                    if part is not None and part + p < ROUTE_PARTS:
                        route(B - 1, part + p)

            row_lo(0, 0)
            rows_t(0, 0)
            for ring in range(RING):
                mlp(ring, ring, 0, ring == 0, False, ring * (HC // 2))
            for ring in range(RING):
                mlp(RING + ring, ring, 1, False, False)
            with dve.Fori(2, NI - 1) as i:
                for ring in range(RING):
                    mlp(i * RING + ring, ring, i, False, False)
            for ring in range(RING):
                mlp(NF - RING + ring, ring, NI - 1, False, ring == RING - 1)
            finish(NF - 1, RING - 1, NI - 1)

        @block.tensor
        def _(pe):
            mm = nc.tensor.matmul
            pe.wait_ge(w_lo, 5)
            pe.wait_ge(consts, 6)
            pe.wait_ge(consts_dve, CONSTS_DVE)
            TERMS = ((0, 0), (0, 1), (1, 0))

            def transpose_y(h):
                pe.wait_ge(ylo_ready, h + 2)
                pe.wait_ge(vlo_ready, h + 1)
                for s in range(2):
                    for c in range(CC):
                        for t in range(QT):
                            at = (s * CC + c) * QB + t * P
                            last = nc.tensor.transpose(f16(p_bank)[:, at:at + P], yhl[:, s, t, c * P:(c + 1) * P],
                                                       ident[:, :])
                last.then_inc(t_done, 1)

            def project_kq(h):
                pe.wait_ge(yt_ready, h + 1)
                for s, w in enumerate((wk_s, wq_s)):
                    for n, (a, c2) in enumerate(TERMS):
                        for c in range(CC):
                            last = mm(p_bank[:, s * QB:(s + 1) * QB], w[:, a, c, :], yt[:, c2, c, :],
                                      start=(n == 0 and c == 0), stop=(n == 2 and c == CC - 1))
                last.then_inc(kq_done, 1)

            def project_v(h):
                pe.wait_ge(kqlo_ready, h + 1)
                for t in range(QT):
                    for n, (a, c2) in enumerate(TERMS):
                        for c in range(CC):
                            last = mm(p_bank[:, t * C:(t + 1) * C], yt[:, a, c, t * P:(t + 1) * P], wv_s[:, c2, c, :],
                                      start=(n == 0 and c == 0), stop=(n == 2 and c == CC - 1))
                last.then_inc(v_done, 1)

            def scores(t, par, nb, j):
                pe.wait_ge(exp_done, t + 1)
                cols = bass.ds(nb * QB, QB)
                for m in range(2):
                    keys = slice((2 * j + m) * P, (2 * j + m + 1) * P)
                    o = s_bank[j % 2][:, m * QB:(m + 1) * QB]
                    mm(o, ka[par][:, keys], qa[par][:, cols], start=True, stop=False)
                    last = mm(o, kb[par][0:D + 1, keys], qb[par][0:D + 1, cols], start=False, stop=True)
                last.then_inc(s_done, 1)

            def unit(k, par, nb, u):
                pe.wait_ge(m_read, k * UNITS + u + 1)
                mm(m_bank[u % 2][:, :], qa[par][:, bass.ds(nb * QB + (u // 8) * P, P)],
                   ka[par][:, (u % 8) * 512:(u % 8 + 1) * 512], start=True, stop=True).then_inc(m_done, 1)

            def max_row(k):
                pe.wait_ge(negm_ready, k + 1)
                for i in range(QT):
                    last = mm(r_bank[D:D + 1, i * P:(i + 1) * P], negm[:, i:i + 1], ident[:, :], start=True, stop=True)
                last.then_inc(row_done, 1)

            def p_v(t, par, j):
                pe.wait_ge(lo_done, t + 3)
                for m in range(2):
                    v_hi1 = vs[par][:, 2 * j + m, 0:C + 1]
                    v_lo = vs[par][:, 2 * j + m, VLO:VLO + C]
                    for i in range(QT):
                        ph = phi[:, j % 4, m, i * P:(i + 1) * P]
                        pl = plo[:, j % 4, m, i * P:(i + 1) * P]
                        begin, end = j == 0 and m == 0, j == STEPS - 1 and m == 1
                        mm(o_bank[i][:, 0:C + 1], ph, v_hi1, start=begin, stop=False, skip_group_check=True)
                        mm(o_bank[i][:, 0:C], ph, v_lo, start=False, stop=False, skip_group_check=True)
                        last = mm(o_bank[i][:, 0:C + 1], pl, v_hi1, start=False, stop=end, skip_group_check=True)
                last.then_inc(pv_done, 1)

            def route_sums(b, e):
                pe.wait_ge(cnt_ready, b * RC_N + e + 1)
                o = r_bank[:, QB:QB + 3 * NT]
                if e < 8:
                    last = mm(o[:, 0:15], ones16[:, :], cnt[:, :], start=True, stop=True)
                elif e == 8:
                    mm(o[:, 0:NT], ones16[:, :], gt16[:, :], start=True, stop=True)
                    mm(o[:, NT:2 * NT], ones16[:, :], eq16[:, :], start=True, stop=True)
                    last = mm(o[:, 2 * NT:3 * NT], tri16[:, :], eq16[:, :], start=True, stop=True)
                else:
                    mm(o[:, 0:NT], ones16[:, :], sel16[:, :], start=True, stop=True)
                    last = mm(o[:, NT:2 * NT], tri16[:, :], sel16[:, :], start=True, stop=True)
                last.then_inc(tot_ready, 1)

            def attend(k, par, nb, following, projects, routed=None):
                u = 0
                for j in range(STEPS):
                    t = k * STEPS + j
                    if j + 2 < STEPS:
                        scores(t + 2, par, nb, j + 2)
                    elif following:
                        if j == STEPS - 2:
                            pe.wait_ge(row_ready, k + 2)
                        scores(t + 2, *following, j + 2 - STEPS)
                    if following:
                        for _ in range(UNIT_OF[j]):
                            unit(k + 1, *following, u)
                            u += 1
                        if j == 13:
                            max_row(k + 1)
                    if j == 0:
                        pe.wait_ge(o_read, k + 1)
                    p_v(t, par, j)
                    if projects:
                        if j == 7:
                            transpose_y(k + AHEAD)
                        elif j == 9:
                            project_kq(k + AHEAD)
                        elif j == 12:
                            project_v(k + AHEAD)
                    if routed and j in ROUTE_AT and routed[1] + ROUTE_AT[j] < RC_N:
                        route_sums(routed[0], routed[1] + ROUTE_AT[j])

            def image_ready(b):
                pe.wait_ge(kqlo_ready, b * NB + NB)
                pe.wait_ge(vlo_ready, b * NB + NB + 1)

            transpose_y(0)
            with pe.Fori(0, NB) as h:
                project_kq(h)
                project_v(h)
                transpose_y(h + 1)
            project_kq(NB)
            project_v(NB)
            image_ready(0)
            for u in range(UNITS):
                unit(0, 0, 0, u)
            max_row(0)
            pe.wait_ge(row_ready, 1)
            for j in range(2):
                scores(j, 0, 0, j)
            for b in range(B):
                par, k0 = b % 2, b * NB
                projects, begin = b < B - 1, 0
                if b > 0:
                    attend(k0, par, 0, (par, 1), projects)
                    for nb, part in ((1, 0), (2, len(ROUTE_AT))):
                        attend(k0 + nb, par, nb, (par, nb + 1), projects, (b - 1, part))
                    begin = 3
                with pe.Fori(begin, NB - 1) as nb:
                    attend(k0 + nb, par, nb, (par, nb + 1), projects)
                if b < B - 1:
                    image_ready(b + 1)
                attend(k0 + NB - 1, par, NB - 1, (1 - par, 0) if projects else None, b < B - 2)

            def transpose_rows(f):
                pe.wait_ge(tlo_ready, f + 1)
                pe.wait_ge(tt_ready, f + 1)
                for h in range(2):
                    for c in range(CC):
                        for t in range(FT):
                            at = (h * CC + c) * FB + t * P
                            last = nc.tensor.transpose(f16(x_bank)[:, at:at + P], thl[:, h, t, c * P:(c + 1) * P],
                                                       ident[:, :])
                last.then_inc(ft_done, 1)

            def hidden(f, ring, p):
                if p == 0:
                    pe.wait_ge(tt_ready, f + 2)
                pe.wait_ge(gelu_done, f * 4 + p + 1)
                for hh in range(2):
                    units = slice((2 * p + hh) * P, (2 * p + hh + 1) * P)
                    for n, (a, c2) in enumerate(TERMS):
                        for c in range(CC):
                            last = mm(h_bank[p % 2][:, hh * FB:(hh + 1) * FB], w1_s[:, a, c, units],
                                      tt[:, ring % 2, c2, c, :], start=(n == 0 and c == 0),
                                      stop=(n == 2 and c == CC - 1))
                last.then_inc(h_done, 1)

            def second(f, ring, p):
                pe.wait_ge(hlo_ready, f * 4 + p + 3)
                if p == 0:
                    pe.wait_ge(y_read, f + 1)
                for hh in range(2):
                    for t in range(FT):
                        o = y_bank[ring % 2][:, t * C:(t + 1) * C]
                        for n, (a, c2) in enumerate(TERMS):
                            h = (hhi, hlo)[a][:, p % 2, hh, t * P:(t + 1) * P]
                            last = mm(o, h, w2_s[:, c2, 2 * p + hh, :], start=(p == hh == t == n == 0),
                                      stop=(p == 3 and hh == 1 and n == 2), skip_group_check=True)
                last.then_inc(w2_done, 1)

            def mlp(f, ring, last, event=None):
                for p in range(HC // 2):
                    if p + 1 < HC // 2:
                        hidden(f, ring, p + 1)
                    elif not last:
                        hidden(f + 1, ring + 1, 0)
                    second(f, ring, p)
                    if p == 1 and not last:
                        transpose_rows(f + 1)
                    if event is not None and event + p < RC_N:
                        route_sums(B - 1, event + p)

            pe.wait_ge(o_read, BLOCKS + 1)
            transpose_rows(0)
            hidden(0, 0, 0)
            for ring in range(RING):
                mlp(ring, ring, False, ring * (HC // 2))
            with pe.Fori(1, NI - 1) as i:
                for ring in range(RING):
                    mlp(i * RING + ring, ring, False)
            for ring in range(RING):
                mlp(NF - RING + ring, ring, ring == RING - 1)


def kernel(**inputs):
    import numpy as np
    import concourse.bacc as bacc
    from concourse.bass_utils import run_bass_kernel_spmd

    a = {k: np.asarray(v) for k, v in inputs.items()}
    wide = lambda v, n: np.ascontiguousarray(np.broadcast_to(v.reshape(1, -1), (P, n)))

    def by_rows(w):
        k, n = w.shape
        return np.ascontiguousarray(w.reshape(k // P, P, n).transpose(1, 0, 2).reshape(P, -1))

    def twice(v):
        return np.ascontiguousarray(np.concatenate([v, v], axis=-1))

    arrays = {
        "x": np.ascontiguousarray(a["x"].reshape(B, C, N).transpose(0, 2, 1).reshape(B * N, C)),
        "wq": by_rows(twice(a["L0_conv_wq"].T)),
        "wk": by_rows(twice(a["L0_conv_wk"].T)),
        "wv": by_rows(a["L0_conv_wv"].T),
        "bq": twice(a["L0_conv_bq"]).reshape(P, 1),
        "bk": twice(a["L0_conv_bk"]).reshape(P, 1),
        "bv": wide(a["L0_conv_bv"], C),
        "wr": wide(a["L0_ffn_wr"], C),
        "br": wide(a["L0_ffn_br"], 1),
        "w1": by_rows(a["L0_ffn_w1"]),
        "b1": np.ascontiguousarray(a["L0_ffn_b1"].reshape(HC, P).T),
        "w2": by_rows(a["L0_ffn_w2"]),
        "b2": wide(a["L0_ffn_b2"], C),
    }
    nc = bacc.Bacc("TRN2", target_bir_lowering=False, num_devices=1)
    args = {k: nc.dram_tensor(f"in_{k}", v.shape, F32, kind="ExternalInput").ap() for k, v in arrays.items()}
    args["out"] = nc.dram_tensor("out_rows", (B * N, C), F32, kind="ExternalOutput").ap()
    build(nc, **args)
    r = run_bass_kernel_spmd(nc, [{f"in_{k}": v for k, v in arrays.items()}], core_ids=[0])
    rows = r.results[0]["out_rows"]
    return np.ascontiguousarray(rows.reshape(B, N, C).transpose(0, 2, 1)).reshape(B, C, 64, 64)
```

```python
from contextlib import ExitStack

import concourse.bass as bass
from concourse import mybir

F32 = mybir.dt.float32
F16 = mybir.dt.float16
I32 = mybir.dt.int32
U32 = mybir.dt.uint32
ALU = mybir.AluOpType
ACT = mybir.ActivationFunctionType
AX = mybir.AxisListType

P = 128
B = 4
N = 4096
C = 256
D = 64
HID = 1024
CC = C // P
HC = HID // P
NT = N // P
KEEP = N // 2
QB = 256
QT = QB // P
NB = N // QB
BLOCKS = B * NB
AHEAD = NB + 1
STEPS = NT // 2
UNITS = QT * (N // 512)
VW = 514
VLO = 258
ROWS = B * KEEP
FB = 256
FT = FB // P
NF = ROWS // FB
RING = 4
NI = NF // RING
MLP_W = CC * HID + HC * C
PAIRS = NB // 2
PIECE = MLP_W // PAIRS
SHIFT = 6.0
UNIT_OF = [1, 1, 1, 1, 1, 1, 1, 1, 2, 1, 2, 1, 0, 0, 1, 1]
UNITS_EARLY = sum(UNIT_OF[-2:])
assert sum(UNIT_OF) == UNITS and len(UNIT_OF) == STEPS
BIG = 100000.0


def build(nc, x, wq, wk, wv, bq, bk, bv, wr, br, w12, b1, b2, ones, out):
    ctx = ExitStack()
    with ctx:
        def sb(name, shape, dt):
            return ctx.enter_context(nc.sbuf_tensor(name, shape, dt))

        def sem(name):
            return ctx.enter_context(nc.semaphore(name))

        packed = nc.dram_tensor("packed", (ROWS, 2), F32, kind="Internal").ap()
        ln_rows = nc.dram_tensor("ln_rows", (B * N, C), F32, kind="Internal").ap()
        x_v = x.rearrange("(k t p) c -> k p t c", p=P, t=QT)
        out_v = out.rearrange("(k t p) c -> k p t c", p=P, t=QT)
        ln_v = ln_rows.rearrange("(k t p) c -> k p t c", p=P, t=QT)
        packed_v = packed.rearrange("(f t p) c -> f p t c", p=P, t=FT)

        ident = sb("ident", [P, P], F16)
        ones16 = sb("ones16", [P, P], F16)
        tri16 = sb("tri16", [P, P], F16)
        wq_s = sb("wq_s", [P, 2, CC, P], F16)
        wk_s = sb("wk_s", [P, 2, CC, P], F16)
        wv_s = sb("wv_s", [P, 2, CC, C], F16)
        w12_s = sb("w12_s", [P, 2, MLP_W], F16)
        w1_s = w12_s[:, :, 0:CC * HID].rearrange("p h (a b) -> p h a b", a=CC)
        w2_s = w12_s[:, :, CC * HID:MLP_W].rearrange("p h (a b) -> p h a b", a=HC)
        bq_s = sb("bq_s", [P, 1], F32)
        bk_s = sb("bk_s", [P, 1], F32)
        br_s = sb("br_s", [P, 1], F32)
        b1_s = sb("b1_s", [P, HC], F32)
        bv_s = sb("bv_s", [P, QT, C], F32)
        wr_s = sb("wr_s", [P, C], F32)
        b2_s = sb("b2_s", [P, FT, C], F32)
        ka = [sb(f"ka{i}", [P, N], F16) for i in range(2)]
        kb = [sb(f"kb{i}", [P, N], F16) for i in range(2)]
        qa = [sb(f"qa{i}", [P, N], F16) for i in range(2)]
        qb = [sb(f"qb{i}", [P, N], F16) for i in range(2)]
        vs = [sb(f"vs{i}", [P, NT, VW], F16) for i in range(2)]
        xp = sb("xp", [P, QT, C], F32)
        xr = sb("xr", [P, QT, C], F32)
        y32 = sb("y32", [P, QT, C], F32)
        yhl = sb("yhl", [P, 2, QT, C], F16)
        yt = sb("yt", [P, 2, CC, QB], F16)
        st = sb("st", [P, QT, 6], F32)
        mv = sb("mv", [P, QT, 2], F32)
        ve = sb("ve", [P, QT], F32)
        rstd = sb("rstd", [P, QT], F32)
        mhalf = sb("mhalf", [P, QT], F32)
        p32 = sb("p32", [P, 4, 2, QB], F32)
        phi = sb("phi", [P, 4, 2, QB], F16)
        plo = sb("plo", [P, 4, 2, QB], F16)
        mpart = sb("mpart", [P, QT, 8], F32)
        mrow = sb("mrow", [P, QT], F32)
        negm = sb("negm", [P, QT], F16)
        oe = sb("oe", [P, QT, C + 1], F32)
        rz = sb("rz", [P, QT], F32)
        tb = sb("tb", [P, QT, C], F32)
        est = sb("est", [P, QT, 6], F32)
        emv = sb("emv", [P, QT, 2], F32)
        eve = sb("eve", [P, QT], F32)
        erstd = sb("erstd", [P, QT], F32)
        wdot = sb("wdot", [P, QT], F32)
        wjunk = sb("wjunk", [P, QT, C], F32)
        lnb = sb("lnb", [P, QT, C], F32)
        res = sb("res", [P, QT, C], F32)
        wcol = sb("wcol", [P, NT], F32)
        wsel = sb("wsel", [P, NT], F32)
        pk = sb("pk", [P, NT, 2], F32)
        tok = sb("tok", [P, NT], I32)
        tokf = sb("tokf", [P, NT], F32)
        rbase = sb("rbase", [P, 1], F32)
        cand_i = sb("cand_i", [P, 15], I32)
        cand1 = sb("cand1", [P, 15], F32)
        keym = sb("keym", [P, NT], I32)
        key = sb("key", [P, NT], I32)
        kpart = sb("kpart", [P, NT], I32)
        khi = sb("khi", [P, NT], F32)
        klo = sb("klo", [P, NT], F32)
        val = sb("val", [P, NT], F32)
        vtmp = sb("vtmp", [P, NT], F32)
        base = sb("base", [P, 2], F32)
        cand = sb("cand", [P, 15], F32)
        cmp = sb("cmp", [P, 15, NT], F32)
        cnt = sb("cnt", [P, 15], F16)
        isge = sb("isge", [P, 15], F32)
        nge = sb("nge", [P, 1], F32)
        gt16 = sb("gt16", [P, NT], F16)
        eq16 = sb("eq16", [P, NT], F16)
        sel16 = sb("sel16", [P, NT], F16)
        csum = sb("csum", [P, NT], F32)
        cexc = sb("cexc", [P, NT], F32)
        zeros = sb("zeros", [P, NT], F32)
        rank = sb("rank", [P, NT], F32)
        need = sb("need", [P, 1], F32)
        ngt = sb("ngt", [P, 1], F32)
        take = sb("take", [P, NT], F32)
        drop = sb("drop", [P, NT], F32)
        rowf = sb("rowf", [P, NT], F32)
        rowi = sb("rowi", [P, NT], I32)
        rowb = sb("rowb", [P, 2, FT, C], F32)
        idw = sb("idw", [P, RING, FT, 2], F32)
        thl = sb("thl", [P, 2, FT, C], F16)
        tt = sb("tt", [P, 2, 2, CC, FB], F16)
        h32, hhi, hlo = p32, phi, plo
        yb = tb
        zb = [xp, y32]

        def halves(b, a):
            return b[:, :, :].rearrange("p t c -> p (t c)").bitcast(F16).rearrange("p (h a n) -> p h a n", h=2, a=a)

        xp2 = [xp, lnb]
        y322 = [y32, tb]
        yhl2 = [yhl, halves(res, QT)]
        yt2 = [yt, halves(wjunk, CC)]

        sizes = [CC * P, CC * P, CC * C]
        starts = [sum(sizes[:i]) for i in range(len(sizes))]
        stage = p32[:, :, :, :].rearrange("p a b c -> p (a b c)")
        staged = [stage[:, a:a + n] for a, n in zip(starts, sizes)]
        split = [w[:, :, :, :].rearrange("p h a b -> p h (a b)") for w in (wq_s, wk_s, wv_s)]
        mlp_stage = vs[1][:, QT:NT, :].rearrange("p a b -> p (a b)").bitcast(F32)

        bank = [ctx.enter_context(nc.psum_tensor(f"bank{i}", [P, 512], F32)) for i in range(8)]
        s_bank = [bank[0], bank[1]]
        m_bank = [bank[2], bank[3]]
        o_bank = [bank[4], bank[5]]
        row_bank = m_bank[0]
        r_bank = bank[6]
        p_bank = bank[7]
        t_bank2, kq_bank2, v_bank2 = s_bank, m_bank, o_bank
        h_bank = [bank[0], bank[1]]
        y_bank = [bank[2], bank[3]]
        x_bank = bank[7]

        def f16(b):
            return b[:, :].bitcast(F16)

        weights_in = sem("weights_in")
        smalls_in = sem("smalls_in")
        mlp_w_in = sem("mlp_w_in")
        first_in = [sem(f"first_in{i}") for i in range(2)]
        xp_in = sem("xp_in")
        xr_in = sem("xr_in")
        consts = sem("consts")
        waits_settled = sem("waits_settled")
        consts_dve = sem("consts_dve")
        w_hi = sem("w_hi")
        w_lo = sem("w_lo")
        var_ready = sem("var_ready")
        dve_p = sem("dve_p")
        rstd_ready = sem("rstd_ready")
        y_ready = sem("y_ready")
        yhi_ready = sem("yhi_ready")
        ylo_ready = sem("ylo_ready")
        t_done = sem("t_done")
        yt_ready = sem("yt_ready")
        kq_done = sem("kq_done")
        kqhi_ready = sem("kqhi_ready")
        kqlo_ready = sem("kqlo_ready")
        v_done = sem("v_done")
        vhi_ready = sem("vhi_ready")
        vlo_ready = sem("vlo_ready")
        s_done = sem("s_done")
        exp_done = sem("exp_done")
        hi_done = sem("hi_done")
        lo_done = sem("lo_done")
        o_done = sem("o_done")
        pv_done = sem("pv_done")
        m_done = sem("m_done")
        m_read = sem("m_read")
        dve_m = sem("dve_m")
        negm_ready = sem("negm_ready")
        row_done = sem("row_done")
        row_ready = sem("row_ready")
        xr_ready = sem("xr_ready")
        o_read = sem("o_read")
        dve_e = sem("dve_e")
        evar_ready = sem("evar_ready")
        erstd_ready = sem("erstd_ready")
        ln_ready = sem("ln_ready")
        ln_out = sem("ln_out")
        w_ready = sem("w_ready")
        res_ready = sem("res_ready")
        res_out = sem("res_out")
        dve_r = sem("dve_r")
        cnt_ready = sem("cnt_ready")
        tot_ready = sem("tot_ready")
        rows_ready = sem("rows_ready")
        pack_out = sem("pack_out")
        id_in = [sem(f"id_in{i}") for i in range(RING)]
        f_in = [sem(f"f_in{i}") for i in range(RING)]
        thi_ready = sem("thi_ready")
        tlo_ready = sem("tlo_ready")
        ft_done = sem("ft_done")
        tt_ready = sem("tt_ready")
        h_done = sem("h_done")
        gelu_done = sem("gelu_done")
        hhi_ready = sem("hhi_ready")
        hlo_ready = sem("hlo_ready")
        w2_done = sem("w2_done")
        y_read = sem("y_read")
        z_ready = sem("z_ready")
        z_out = [sem(f"z_out{i}") for i in range(RING)]

        E_N = 9
        P_N = 2 * QT
        own_order = [0]
        PIECES = (4, 3, 3, 3, 4, 3, 3, 3, 2, 3, 2)
        ROUTE_PARTS = len(PIECES)
        route_from = [sum(PIECES[:i]) + i for i in range(ROUTE_PARTS)]
        ROUTE_AT = {route_from[i] + n: (i, n) for i in range(ROUTE_PARTS) for n in range(PIECES[i])}
        SUMS_AT = {route_from[i] + (2 if i == 9 else PIECES[i]): i for i in range(ROUTE_PARTS - 1)}
        ROUTE_STEPS = (1, 4, 5, 6, 9, 10, 12, 13, 14, 15)
        ROUTE_BLOCKS = -(-(max(ROUTE_AT) + 1) // len(ROUTE_STEPS))

        def routing_at(table, block, j):
            if j in ROUTE_STEPS:
                return table.get(block * len(ROUTE_STEPS) + ROUTE_STEPS.index(j))
            return None
        ROUTED_BY = -(-((max(ROUTE_AT) + 1) // (HC // 2) + 1) // RING)
        assert (ROUTED_BY + 2) * RING <= NF - NF // B - 2
        RC_N = 10

        WEIGHTS = 5 * 16
        SMALLS = 9 * 16
        CONSTS_DVE = 7

        def settled(eng):
            eng.sem_inc(waits_settled, 1)

        block = ctx.enter_context(nc.Block())

        @block.sync
        def _(sp):
            def of_block(view, k):
                return view[bass.ds(k, 1)].rearrange("k p t c -> p (k t) c")

            def load_first(h, r):
                if not isinstance(h, int) or h > 0:
                    sp.wait_ge(y_ready, h * QT)
                sp.dma_start(xp2[r][:, :, :], of_block(x_v, h)).then_inc(first_in[r], 16)

            def load_projected(h):
                sp.wait_ge(y_ready, h * QT + QT)
                sp.dma_start(xp[:, :, :], of_block(x_v, h)).then_inc(xp_in, 16)

            def load_piece(i):
                sp.wait_ge(w_hi, len(split) + i)
                cols = bass.ds(i * PIECE, PIECE)
                sp.dma_start(mlp_stage[:, cols], w12[:, cols]).then_inc(mlp_w_in, 16)

            def load_residual(k):
                sp.wait_ge(dve_e, k * E_N + 3)
                sp.dma_start(xr[:, :, :], of_block(x_v, k)).then_inc(xr_in, 16)

            def store_ln(k):
                sp.wait_ge(ln_ready, k * QT + QT)
                sp.dma_start(of_block(ln_v, k), lnb[:, :, :]).then_inc(ln_out, 16)

            def store_sum(k):
                sp.wait_ge(res_ready, k + 2)
                sp.dma_start(of_block(out_v, k), res[:, :, :]).then_inc(res_out, 16)

            load_first(0, 0)
            for i, w in enumerate((wq, wk, wv)):
                sp.dma_start(staged[i], w).then_inc(weights_in, 16)
            for s, w in ((bq_s, bq), (bk_s, bk)):
                sp.dma_start(s[:, :], w).then_inc(weights_in, 16)
            load_first(1, 1)
            with sp.Fori(1, PAIRS) as i:
                for r in range(2):
                    load_first(2 * i + r, r)
                load_piece(i - 1)
            load_first(NB, 0)
            load_piece(PAIRS - 1)
            for i in range(2):
                sp.dma_start(kb[i][D:D + 1, :], ones).then_inc(smalls_in, 16)
            for s, w in ((br_s, br), (b1_s, b1), (wr_s, wr)):
                sp.dma_start(s[:, :], w).then_inc(smalls_in, 16)
            for s, w in ((bv_s, bv), (b2_s, b2)):
                for i in range(2):
                    sp.dma_start(s[:, i, :], w).then_inc(smalls_in, 16)
            load_projected(AHEAD)
            load_residual(0)
            load_projected(AHEAD + 1)
            with sp.Fori(1, BLOCKS - AHEAD - 1) as k:
                load_residual(k)
                load_projected(k + AHEAD + 1)
                store_ln(k - 1)
                store_sum(k - 1)
            with sp.Fori(BLOCKS - AHEAD - 1, BLOCKS) as k:
                load_residual(k)
                store_ln(k - 1)
                store_sum(k - 1)

            sp.wait_ge(pack_out, (B - 1) * NT * 16)

            def load_ids(f, ring):
                sp.dma_start(idw[:, ring, :, :],
                             packed_v[bass.ds(f, 1)].rearrange("f p t c -> p (f t) c")).then_inc(id_in[ring], 16)

            def load_ids_of(i):
                for ring in range(RING):
                    sp.wait_ge(z_out[ring], i * (FT * 16))
                    load_ids(i * RING + ring, ring)

            for ring in range(RING):
                load_ids(ring, ring)
            store_ln(BLOCKS - 1)
            store_sum(BLOCKS - 1)
            with sp.Fori(1, NI - NI // B) as i:
                load_ids_of(i)
            sp.wait_ge(pack_out, B * NT * 16)
            with sp.Fori(NI - NI // B, NI) as i:
                load_ids_of(i)
            sp.wait_ge(ln_out, BLOCKS * 16 + 16)
            sp.wait_ge(res_out, BLOCKS * 16 + 16)
            for ring in range(RING):
                sp.wait_ge(z_out[ring], NI * FT * 16)

        @block.gpsimd
        def _(pool):
            G = nc.gpsimd
            G.memset(ident[:, :], 0.0).then_inc(consts, 1)
            G.memset(tri16[:, :], 0.0).then_inc(consts, 1)
            G.iota(tok[:, :], pattern=[[P, NT]], base=0, channel_multiplier=1).then_inc(consts, 1)
            G.iota(cand_i[:, :], pattern=[[1, 15]], base=1, channel_multiplier=0).then_inc(consts, 1)
            pool.wait_ge(consts, 4)
            G.affine_select(out=ident[:, :], in_=ident[:, :], compare_op=ALU.not_equal, fill=1.0,
                            base=0, pattern=[[-1, P]], channel_multiplier=1).then_inc(consts, 1)
            G.affine_select(out=tri16[:, :], in_=tri16[:, :], compare_op=ALU.is_ge, fill=1.0,
                            base=0, pattern=[[-1, P]], channel_multiplier=1).then_inc(consts, 1)

            def project_rstd(h):
                pool.wait_ge(var_ready, h + 1)
                G.tensor_tensor(rstd[:, :], ve[:, :], mhalf[:, :], ALU.pow).then_inc(rstd_ready, 1)

            def first_lo(h, r):
                pool.wait_ge(yhi_ready, h + 1)
                if not isinstance(h, int) or h > 0:
                    pool.wait_ge(t_done, h)
                G.tensor_tensor(yhl2[r][:, 1, :, :], y322[r][:, :, :], yhl2[r][:, 0, :, :], ALU.subtract
                                ).then_inc(ylo_ready, 1)

            def project_lo(h):
                pool.wait_ge(yhi_ready, h + 1)
                pool.wait_ge(t_done, h + 1)
                G.tensor_tensor(yhl[:, 1, :, :], y32[:, :, :], yhl[:, 0, :, :], ALU.subtract).then_inc(ylo_ready, 1)

            def end_rstd(k):
                pool.wait_ge(evar_ready, k + 1)
                G.tensor_tensor(erstd[:, :], eve[:, :], mhalf[:, :], ALU.pow).then_inc(erstd_ready, 1)

            def residual(k):
                pool.wait_ge(xr_in, k * 16 + 16)
                G.tensor_tensor(xr[:, :, :], xr[:, :, :], bv_s[:, :, :], ALU.add).then_inc(xr_ready, 1)

            def end_sum(k):
                pool.wait_ge(ln_ready, k * QT + QT)
                pool.wait_ge(res_out, k * 16 + 16)
                G.tensor_tensor(res[:, :, :], tb[:, :, :], lnb[:, :, :], ALU.add).then_inc(res_ready, 1)

            def pack(tiles):
                for t in tiles:
                    G.indirect_dma_start(
                        out=packed, out_offset=bass.IndirectOffsetOnAxis(ap=rowi[:, t:t + 1].bitcast(U32), axis=0),
                        in_=pk[:, t, :], in_offset=None, bounds_check=ROWS - 1, oob_is_err=False,
                    ).then_inc(pack_out, 16)

            def attend(k, first, projects):
                if projects:
                    project_rstd(k + AHEAD)
                if not first:
                    end_rstd(k - 1)
                residual(k)
                if projects:
                    project_lo(k + AHEAD)
                if not first:
                    end_sum(k - 1)

            pool.wait_ge(consts_dve, CONSTS_DVE)
            project_rstd(0)
            project_rstd(1)
            for h in range(2):
                first_lo(h, h)
                project_rstd(h + 2)
            with pool.Fori(1, PAIRS - 1) as i:
                for r in range(2):
                    first_lo(2 * i + r, r)
                    project_rstd(2 * i + r + 2)
            first_lo(NB - 2, 0)
            project_rstd(NB)
            first_lo(NB - 1, 1)
            first_lo(NB, 0)
            pool.wait_ge(smalls_in, SMALLS)
            attend(0, True, True)
            with pool.Fori(1, NB) as k:
                attend(k, False, True)
            for b in range(1, B):
                for nb in range(1 + ROUTE_BLOCKS):
                    attend(b * NB + nb, False, b < B - 1)
                pool.wait_ge(rows_ready, b)
                for n in range(NT // 4):
                    pack(range(n * 4, n * 4 + 4))
                    attend(b * NB + 1 + ROUTE_BLOCKS + n, False, b < B - 1)
                pool.wait_ge(pack_out, b * NT * 16)
                with pool.Fori(1 + ROUTE_BLOCKS + NT // 4, NB - 1) as nb:
                    attend(b * NB + nb, False, b < B - 1)
                attend(b * NB + NB - 1, False, b < B - 2)

            def gather(f, i, ring, images=B):
                pool.wait_ge(id_in[ring], i * 16 + 16)
                if not (isinstance(f, int) and f < 2):
                    pool.wait_ge(tlo_ready, f - 1)
                    settled(pool)
                for t in range(FT):
                    G.indirect_dma_start(
                        out=rowb[:, ring % 2, t, :], out_offset=None, in_=ln_rows[0:images * N, :],
                        in_offset=bass.IndirectOffsetOnAxis(ap=idw[:, ring, t, 1:2].bitcast(U32), axis=0),
                        bounds_check=images * N - 1,
                    ).then_inc(f_in[ring], 16)

            def scatter(f, ring):
                pool.wait_ge(z_ready, f * FT + FT)
                settled(pool)
                for t in range(FT):
                    G.indirect_dma_start(
                        out=out,
                        out_offset=bass.IndirectOffsetOnAxis(ap=idw[:, ring, t, 1:2].bitcast(U32), axis=0),
                        in_=zb[ring % 2][:, t, :], in_offset=None, bounds_check=B * N - 1, compute_op=ALU.add,
                    ).then_inc(z_out[ring], 16)

            def mlp(i, packs, last):
                for ring in range(RING):
                    if not (last and ring >= RING - 2) and not (isinstance(i, int) and i == ring == 0):
                        gather(i * RING + ring + 2, i + (ring + 2) // RING, (ring + 2) % RING)
                    if packs is not None:
                        pack(range(packs + ring * 4, packs + ring * 4 + 4))
                    scatter(i * RING + ring, ring)

            pool.wait_ge(ln_out, (B - 1) * NB * 16 + 16)
            gather(0, 0, 0, B - 1)
            gather(1, 0, 1, B - 1)
            gather(2, 0, 2, B - 1)
            end_rstd(BLOCKS - 1)
            end_sum(BLOCKS - 1)
            pool.wait_ge(ln_out, BLOCKS * 16 + 16)
            pool.wait_ge(res_out, BLOCKS * 16 + 16)
            for i in range(ROUTED_BY):
                mlp(i, None, False)
            pool.wait_ge(rows_ready, B)
            for n in range(2):
                mlp(ROUTED_BY + n, n * 16, False)
            with pool.Fori(ROUTED_BY + 2, NI - 1) as i:
                mlp(i, None, False)
            mlp(NI - 1, None, True)

        @block.scalar
        def _(act):
            A = nc.scalar
            def first_y_hi(h, r):
                act.wait_ge(y_ready, h * QT + QT + 2)
                if not isinstance(h, int) or h > 0:
                    act.wait_ge(t_done, h)
                A.copy(yhl2[r][:, 0, :, :], y322[r][:, :, :]).then_inc(yhi_ready, 1)

            def first_y_t(h, r):
                act.wait_ge(t_done, h + 2)
                A.copy(yt2[r][:, :, :, :].rearrange("p h c n -> p (h c n)"), f16(t_bank2[r])).then_inc(yt_ready, 1)

            def y_hi(h):
                act.wait_ge(y_ready, h * QT + QT + 2)
                act.wait_ge(t_done, h + 1)
                A.copy(yhl[:, 0, :, :], y32[:, :, :]).then_inc(yhi_ready, 1)

            def y_t(h):
                act.wait_ge(t_done, h + 2)
                A.copy(yt[:, :, :, :].rearrange("p h c n -> p (h c n)"), f16(p_bank)).then_inc(yt_ready, 1)

            def kq_hi(h, par, nb, kq_bank=p_bank):
                cols = bass.ds(nb * QB, QB)
                act.wait_ge(kq_done, h + 1)
                A.activation(ka[par][:, cols], kq_bank[:, 0:QB], ACT.Identity, bias=bk_s[:, 0:1])
                A.activation(qb[par][:, cols], kq_bank[:, QB:2 * QB], ACT.Identity, bias=bq_s[:, 0:1])
                A.activation(qa[par][0:D, cols], kq_bank[0:D, QB:2 * QB], ACT.Identity, bias=bq_s[0:D, 0:1]
                             ).then_inc(kqhi_ready, 1)

            def v_hi(h, par, nb, v_bank=p_bank):
                act.wait_ge(v_done, h + 1)
                A.copy(vs[par][:, bass.ds(nb * QT, QT), 0:C], v_bank[:, :].rearrange("p (t c) -> p t c", t=QT)
                       ).then_inc(vhi_ready, 1)

            def exponent(t, j):
                act.wait_ge(s_done, t + 1)
                act.wait_ge(lo_done, t + 1)
                A.activation(p32[:, j % 4, :, :].rearrange("p m n -> p (m n)"), s_bank[j % 2][:, :], ACT.Exp
                             ).then_inc(exp_done, 1)

            def p_hi(t, j):
                act.wait_ge(exp_done, t + 3)
                act.wait_ge(pv_done, t + 1)
                A.copy(phi[:, j % 4, :, :], p32[:, j % 4, :, :]).then_inc(hi_done, 1)

            def evacuate(k):
                act.wait_ge(o_done, k + 1)
                A.copy(oe[:, 0, :], o_bank[0][:, 0:C + 1]).then_inc(o_read, 1)
                act.wait_ge(pv_done, k * STEPS + STEPS + 4)
                A.copy(oe[:, 1, :], o_bank[1][:, 0:C + 1]).then_inc(o_read, 1)

            def row(k, par, nb):
                act.wait_ge(row_done, k + 1)
                A.copy(qb[par][D:D + 1, bass.ds(nb * QB, QB)], row_bank[D:D + 1, 0:QB]).then_inc(row_ready, 1)

            def attend(k, following, projected, first=False):
                for j in range(STEPS):
                    t = k * STEPS + j
                    p_hi(t, j)
                    if j + 1 < STEPS or following:
                        exponent(t + 1, (j + 1) % STEPS)
                    if j == 0 and not first:
                        evacuate(k - 1)
                    if j == 13 and following:
                        row(k + 1, *following)
                    if projected:
                        if j == 5:
                            y_hi(k + AHEAD)
                        elif j == 9:
                            y_t(k + AHEAD)
                        elif j == 11:
                            kq_hi(k + AHEAD, *projected)
                        elif j == 15:
                            v_hi(k + AHEAD, *projected)

            def first(h, r, behind):
                if behind > 1:
                    first_y_hi(h + 2, r)
                first_y_t(h + 1, 1 - r)
                kq_hi(h, 0, h, kq_bank2[r])
                v_hi(h, 0, h, v_bank2[r])

            def piece_hi(i):
                act.wait_ge(mlp_w_in, i * 16 + 16)
                cols = bass.ds(i * PIECE, PIECE)
                A.copy(w12_s[:, 0, cols], mlp_stage[:, cols]).then_inc(w_hi, 1)

            first_y_hi(0, 0)
            act.wait_ge(weights_in, WEIGHTS)
            for s, w in zip(staged, split):
                A.copy(w[:, 0, :], s).then_inc(w_hi, 1)
            first_y_t(0, 0)
            first_y_hi(1, 1)
            with act.Fori(0, PAIRS - 1) as i:
                for r in range(2):
                    first(2 * i + r, r, NB)
                piece_hi(i)
            for r in range(2):
                first(NB - 2 + r, r, 2 - r)
            piece_hi(PAIRS - 1)
            kq_hi(NB, 1, 0, kq_bank2[0])
            v_hi(NB, 1, 0, v_bank2[0])
            row(0, 0, 0)
            exponent(0, 0)
            for b in range(B):
                par, k0 = b % 2, b * NB
                if b == 0:
                    attend(0, (par, 1), (1 - par, 1), first=True)
                with act.Fori(b == 0, NB - 1) as nb:
                    attend(k0 + nb, (par, nb + 1), (1 - par, nb + 1) if b < B - 1 else None)
                attend(k0 + NB - 1, (1 - par, 0) if b < B - 1 else None, (par, 0) if b < B - 2 else None)

            def row_hi(f, ring, i):
                act.wait_ge(f_in[ring], (i + 1) * (FT * 16))
                act.wait_ge(ft_done, f + 1)
                A.copy(thl[:, 0, :, :], rowb[:, ring % 2, :, :]).then_inc(thi_ready, 1)

            def mlp(f, ring, i, last):
                for p in range(HC // 2):
                    q = f * (HC // 2) + p
                    act.wait_ge(h_done, q + 1)
                    act.wait_ge(hlo_ready, q + 1)
                    A.activation(h32[:, p % 2, 0, :], h_bank[p % 2][:, 0:FB], ACT.Gelu_apprx_tanh,
                                 bias=b1_s[:, 2 * p:2 * p + 1])
                    A.activation(h32[:, p % 2, 1, :], h_bank[p % 2][:, FB:2 * FB], ACT.Gelu_apprx_tanh,
                                 bias=b1_s[:, 2 * p + 1:2 * p + 2]).then_inc(gelu_done, 1)
                    act.wait_ge(gelu_done, q + 3)
                    act.wait_ge(w2_done, q + 1)
                    A.copy(hhi[:, p % 2, :, :], h32[:, p % 2, :, :]).then_inc(hhi_ready, 1)
                    if p == 0 and not last:
                        row_hi(f + 1, (ring + 1) % RING, i + (ring + 1) // RING)

            row_hi(0, 0, 0)
            evacuate(BLOCKS - 1)
            with act.Fori(0, NI - 1) as i:
                for ring in range(RING):
                    mlp(i * RING + ring, ring, i, False)
            for ring in range(RING):
                mlp(NF - RING + ring, ring, NI - 1, ring == RING - 1)

        @block.vector
        def _(dve):
            V = nc.vector
            for s, n in ((y_ready, 2), (ylo_ready, 1), (t_done, 1), (vlo_ready, 1), (exp_done, 2), (lo_done, 4),
                         (pv_done, 4), (m_read, 2), (o_read, QT), (dve_e, E_N), (res_ready, 1), (ln_out, 16),
                         (res_out, 16), (ft_done, 1), (tt_ready, 1), (gelu_done, 2), (hlo_ready, 2), (w2_done, 2),
                         (y_read, 2)):
                dve.sem_inc(s, n)
            V.memset(ones16[:, :], 1.0).then_inc(consts_dve, 1)
            V.memset(mhalf[:, :], -0.5).then_inc(consts_dve, 1)
            V.memset(zeros[:, :], 0.0).then_inc(consts_dve, 1)
            V.memset(rbase[:, :], 0.0).then_inc(consts_dve, 1)
            dve.wait_ge(consts, 6)
            V.tensor_copy(cand1[:, :], cand_i[:, :]).then_inc(consts_dve, 1)
            V.tensor_copy(tokf[:, :], tok[:, :]).then_inc(consts_dve, 1)
            V.memset(vs[0][:, :, C:C + 1], 1.0).then_inc(consts_dve, 1)

            def first_variance(i, r):
                dve.wait_ge(first_in[r], i * 16 + 16)
                for t in range(QT):
                    V.bn_stats(st[:, t, :], xp2[r][:, t, :]).then_inc(dve_p, 1)

            def variance(h):
                dve.wait_ge(xp_in, (h - AHEAD) * 16 + 16)
                for t in range(QT):
                    V.bn_stats(st[:, t, :], xp[:, t, :]).then_inc(dve_p, 1)

            def var_eps(h):
                dve.wait_ge(dve_p, h * P_N + QT)
                settled(dve)
                for t in range(QT):
                    V.bn_aggr(mv[:, t, :], st[:, t, :]).then_inc(dve_p, 1)
                dve.wait_ge(dve_p, h * P_N + 2 * QT)
                V.tensor_scalar(ve[:, :], mv[:, :, 1], 1e-6, None, ALU.add).then_inc(var_ready, 1)

            def normalise(h):
                dve.wait_ge(rstd_ready, h + 1)
                dve.wait_ge(ylo_ready, h + 1)
                for t in range(QT):
                    V.tensor_scalar(y32[:, t, :], xp[:, t, :], mv[:, t, 0:1], rstd[:, t:t + 1],
                                    ALU.subtract, ALU.mult).then_inc(y_ready, 1)

            def first_normalise(h, r):
                dve.wait_ge(rstd_ready, h + 1)
                if not isinstance(h, int) or h > 0:
                    dve.wait_ge(ylo_ready, h)
                for t in range(QT):
                    V.tensor_scalar(y322[r][:, t, :], xp2[r][:, t, :], mv[:, t, 0:1], rstd[:, t:t + 1],
                                    ALU.subtract, ALU.mult).then_inc(y_ready, 1)

            def kq_lo(h, par, nb, kq_bank=p_bank):
                cols = bass.ds(nb * QB, QB)
                dve.wait_ge(kqhi_ready, h + 1)
                V.scalar_tensor_tensor(out=kb[par][0:D, cols], in0=kq_bank[0:D, 0:QB], scalar=bk_s[0:D, 0:1],
                                       in1=ka[par][0:D, cols], op0=ALU.add, op1=ALU.subtract)
                V.scalar_tensor_tensor(out=qa[par][D:2 * D, cols], in0=kq_bank[D:2 * D, QB:2 * QB],
                                       scalar=bq_s[D:2 * D, 0:1], in1=qb[par][D:2 * D, cols],
                                       op0=ALU.add, op1=ALU.subtract).then_inc(kqlo_ready, 1)

            def v_lo(h, par, nb, v_bank=p_bank):
                dve.wait_ge(vhi_ready, h + 1)
                tiles = bass.ds(nb * QT, QT)
                V.tensor_tensor(vs[par][:, tiles, VLO:VLO + C], v_bank[:, :].rearrange("p (t c) -> p t c", t=QT),
                                vs[par][:, tiles, 0:C], ALU.subtract).then_inc(vlo_ready, 1)

            def p_lo(t, j):
                dve.wait_ge(hi_done, t + 1)
                V.tensor_tensor(plo[:, j % 4, :, :], p32[:, j % 4, :, :], phi[:, j % 4, :, :],
                                ALU.subtract).then_inc(lo_done, 1)

            def unit_max(k, u):
                dve.wait_ge(m_done, k * UNITS + u + 1)
                V.tensor_reduce(mpart[:, u // 8, u % 8:u % 8 + 1], m_bank[u % 2][:, :], AX.X, ALU.max
                                ).then_inc(m_read, 1)

            def row_max(k):
                dve.wait_ge(m_read, k * UNITS + UNITS + 2)
                V.tensor_reduce(mrow[:, :], mpart[:, :, :], AX.X, ALU.max).then_inc(dve_m, 1)
                dve.wait_ge(dve_m, k + 1)
                V.tensor_scalar(negm[:, :], mrow[:, :], -1.0, SHIFT, ALU.mult, ALU.add).then_inc(negm_ready, 1)

            def end_block(k, nb, part):
                e0 = k * E_N + E_N
                if part == 0:
                    dve.wait_ge(o_read, k * QT + 2 * QT)
                    V.reciprocal(rz[:, :], oe[:, :, C]).then_inc(dve_e, 1)
                elif part == 1:
                    dve.wait_ge(dve_e, e0 + 1)
                    dve.wait_ge(xr_ready, k + 1)
                    dve.wait_ge(res_ready, k + 1)
                    for i in range(QT):
                        V.scalar_tensor_tensor(out=tb[:, i, :], in0=oe[:, i, 0:C], scalar=rz[:, i:i + 1],
                                               in1=xr[:, i, :], op0=ALU.mult, op1=ALU.add).then_inc(dve_e, 1)
                elif part == 2:
                    dve.wait_ge(dve_e, e0 + 3)
                    for i in range(QT):
                        V.bn_stats(est[:, i, :], tb[:, i, :]).then_inc(dve_e, 1)
                elif part == 3:
                    dve.wait_ge(dve_e, e0 + 5)
                    settled(dve)
                    for i in range(QT):
                        V.bn_aggr(emv[:, i, :], est[:, i, :]).then_inc(dve_e, 1)
                    dve.wait_ge(dve_e, e0 + 7)
                    V.tensor_scalar(eve[:, :], emv[:, :, 1], 1e-5, None, ALU.add).then_inc(evar_ready, 1)
                elif part == 4:
                    dve.wait_ge(erstd_ready, k + 1)
                    dve.wait_ge(ln_out, k * 16 + 16)
                    for i in range(QT):
                        V.tensor_scalar(lnb[:, i, :], tb[:, i, :], emv[:, i, 0:1], erstd[:, i:i + 1],
                                        ALU.subtract, ALU.mult).then_inc(ln_ready, 1)
                elif part == 5:
                    dve.wait_ge(ln_ready, k * QT + QT)
                    for i in range(QT):
                        V.tensor_tensor_reduce(out=wjunk[:, i, :], in0=lnb[:, i, :], in1=wr_s[:, :], scale=1.0,
                                               scalar=0.0, op0=ALU.mult, op1=ALU.add, accum_out=wdot[:, i:i + 1]
                                               ).then_inc(dve_e, 1)
                elif part == 6:
                    dve.wait_ge(dve_e, e0 + 9)
                    V.tensor_scalar(wcol[:, bass.ds(nb * QT, QT)], wdot[:, :], br_s[:, 0:1], None, ALU.add
                                    ).then_inc(w_ready, 1)

            PART_AT = {1: 0, 2: 1, 4: 2, 5: 3, 7: 4, 8: 5, 9: 6}

            def attend(k, ahead, projected, ended, routed=None):
                u = UNITS_EARLY - UNIT_OF[-1]
                for j in range(STEPS):
                    p_lo(k * STEPS + j, j)
                    if j < STEPS - 1 and ahead > 0:
                        for _ in range(UNIT_OF[j - 1]):
                            unit_max(k + 1, u)
                            u += 1
                        if UNIT_OF[j - 1] and u == UNITS:
                            row_max(k + 1)
                    elif j == STEPS - 1 and ahead > 1:
                        for u in range(UNIT_OF[j - 1]):
                            unit_max(k + 2, u)
                    if j in PART_AT and ended is not None:
                        end_block(k - 1, ended, PART_AT[j])
                    if projected:
                        if j == 0:
                            variance(k + AHEAD)
                        elif j == 1:
                            var_eps(k + AHEAD)
                        elif j == 3:
                            normalise(k + AHEAD)
                        elif j == 12:
                            kq_lo(k + AHEAD, *projected)
                        elif j == 15:
                            v_lo(k + AHEAD, *projected)
                    if routed and routing_at(ROUTE_AT, routed[1], j):
                        part, piece = routing_at(ROUTE_AT, routed[1], j)
                        route(routed[0], part, (piece,))

            def route(b, part, pieces):

                def own(ins):
                    ins.then_inc(dve_r, 1)
                    own_order[0] += 1
                    dve.wait_ge(dve_r, own_order[0])

                def candidates(col, step):
                    own(V.tensor_scalar(cand[:, :], cand1[:, :], step, base[:, col:col + 1], ALU.mult, ALU.add))

                def compare(vals):
                    own(V.tensor_tensor(cmp[:, :, :], vals[:, :].unsqueeze(1).to_broadcast([P, 15, NT]),
                                        cand[:, :].unsqueeze(2).to_broadcast([P, 15, NT]), ALU.is_ge))

                def count():
                    with nc.allow_low_precision(reason="counts up to 32 are exact"):
                        V.tensor_reduce(cnt[:, :], cmp[:, :, :], AX.X, ALU.add).then_inc(cnt_ready, 1)

                def advance(col, step):
                    own(V.tensor_scalar(isge[:, :], sums[:, 0:15], KEEP - 0.5, None, ALU.is_ge))
                    own(V.tensor_reduce(nge[:, :], isge[:, :], AX.X, ALU.add))
                    own(V.scalar_tensor_tensor(out=base[:, col:col + 1], in0=nge[:, :], scalar=step,
                                               in1=base[:, col:col + 1], op0=ALU.mult, op1=ALU.add))

                def rank_of(col_sums, prefix):
                    own(V.tensor_tensor_scan(csum[:, :], zeros[:, :], col_sums, 0.0, ALU.add, ALU.add))
                    own(V.tensor_tensor(cexc[:, :], csum[:, :], col_sums, ALU.subtract))
                    own(V.tensor_tensor(rank[:, :], cexc[:, :], prefix, ALU.add))

                sums = r_bank[:, 0:3 * NT]
                steps = (4096.0, 256.0, 16.0, 1.0)
                for piece in pieces:
                    if part > 0 and piece == 0:
                        dve.wait_ge(tot_ready, b * RC_N + part)
                    if part < 8 and piece >= PIECES[part] - 2:
                        if piece == PIECES[part] - 2:
                            compare(khi if part < 4 else val)
                        else:
                            count()
                    elif part == 0 and piece == 0:
                        dve.wait_ge(w_ready, (b + 1) * NB)
                        own(V.tensor_copy(wsel[:, :], wcol[:, :]))
                        w_i = wsel[:, :].bitcast(I32)
                        own(V.tensor_scalar(keym[:, :], w_i, 31, -2147483648, ALU.arith_shift_right, ALU.bitwise_or))
                        own(V.tensor_tensor(key[:, :], w_i, keym[:, :], ALU.bitwise_xor))
                        own(V.tensor_scalar(kpart[:, :].bitcast(U32), key[:, :].bitcast(U32), 16, None,
                                            ALU.logical_shift_right))
                    elif part == 0:
                        own(V.tensor_copy(khi[:, :], kpart[:, :]))
                        own(V.tensor_scalar(kpart[:, :], key[:, :], 65535, None, ALU.bitwise_and))
                        own(V.tensor_copy(klo[:, :], kpart[:, :]))
                        own(V.memset(base[:, :], 0.0))
                        candidates(0, steps[0])
                    elif part < 4:
                        advance(0, steps[part - 1])
                        candidates(0, steps[part])
                    elif part == 4 and piece == 0:
                        advance(0, steps[3])
                    elif part == 4:
                        own(V.tensor_scalar(vtmp[:, :], klo[:, :], 1.0, None, ALU.add))
                        own(V.scalar_tensor_tensor(out=vtmp[:, :], in0=khi[:, :], scalar=base[:, 0:1], in1=vtmp[:, :],
                                                   op0=ALU.is_equal, op1=ALU.mult))
                        own(V.tensor_scalar(val[:, :], khi[:, :], base[:, 0:1], 70000.0, ALU.is_gt, ALU.mult))
                        own(V.scalar_tensor_tensor(out=val[:, :], in0=val[:, :], scalar=-1.0, in1=vtmp[:, :],
                                                   op0=ALU.add, op1=ALU.add))
                        candidates(1, steps[0])
                    elif part < 8:
                        advance(1, steps[part - 5])
                        candidates(1, steps[part - 4])
                    elif part == 8 and piece == 0:
                        advance(1, steps[3])
                    elif part == 8:
                        own(V.tensor_scalar(gt16[:, :], val[:, :], base[:, 1:2], None, ALU.is_gt))
                        V.tensor_scalar(eq16[:, :], val[:, :], base[:, 1:2], None, ALU.is_equal).then_inc(cnt_ready, 1)
                    elif part == 9 and piece == 0:
                        own(V.tensor_reduce(ngt[:, :], sums[:, 0:NT], AX.X, ALU.add))
                        own(V.tensor_scalar(need[:, :], ngt[:, :], -1.0, float(KEEP), ALU.mult, ALU.add))
                        rank_of(sums[:, NT:2 * NT], sums[:, 2 * NT:3 * NT])
                    elif part == 9 and piece == 1:
                        own(V.scalar_tensor_tensor(out=take[:, :], in0=rank[:, :], scalar=need[:, 0:1],
                                                   in1=eq16[:, :], op0=ALU.is_lt, op1=ALU.mult))
                        V.tensor_tensor(sel16[:, :], take[:, :], gt16[:, :], ALU.add).then_inc(cnt_ready, 1)
                    elif part == 9:
                        own(V.tensor_scalar(drop[:, :], rank[:, :], 1.0, need[:, 0:1], ALU.add, ALU.is_equal))
                        own(V.tensor_tensor(drop[:, :], drop[:, :], eq16[:, :], ALU.mult))
                        own(V.tensor_scalar(drop[:, :], drop[:, :], -1.0, 1.0, ALU.mult, ALU.add))
                        own(V.tensor_tensor(pk[:, :, 0], wsel[:, :], drop[:, :], ALU.mult))
                        own(V.tensor_copy(pk[:, :, 1].bitcast(I32), tokf[:, :]))
                        own(V.tensor_scalar(tokf[:, :], tokf[:, :], float(N), None, ALU.add))
                    elif piece == 0:
                        rank_of(sums[:, 0:NT], sums[:, NT:2 * NT])
                    else:
                        own(V.scalar_tensor_tensor(out=rowf[:, :], in0=rank[:, :], scalar=rbase[:, 0:1],
                                                   in1=sel16[:, :], op0=ALU.add, op1=ALU.mult))
                        own(V.tensor_scalar(take[:, :], sel16[:, :], -BIG, BIG, ALU.mult, ALU.add))
                        own(V.tensor_tensor(rowf[:, :], rowf[:, :], take[:, :], ALU.add))
                        own(V.tensor_scalar(rbase[:, :], rbase[:, :], float(KEEP), None, ALU.add))
                        V.tensor_copy(rowi[:, :], rowf[:, :]).then_inc(rows_ready, 1)

            def first(i, r, behind):
                h = 2 * i + r
                if behind > 2:
                    first_normalise(h + 3, 1 - r)
                kq_lo(h, 0, h, kq_bank2[r])
                if behind > 3:
                    first_variance(i + 2, r)
                    var_eps(h + 4)
                v_lo(h, 0, h, v_bank2[r])

            def piece_lo(i):
                dve.wait_ge(w_hi, len(split) + i + 1)
                cols = bass.ds(i * PIECE, PIECE)
                V.tensor_tensor(w12_s[:, 1, cols], mlp_stage[:, cols], w12_s[:, 0, cols], ALU.subtract
                                ).then_inc(w_lo, 1)

            for h in range(2):
                first_variance(0, h)
                var_eps(h)
                first_normalise(h, h)
            first_variance(1, 0)
            var_eps(2)
            for n, (s, w) in enumerate(zip(staged, split)):
                dve.wait_ge(w_hi, n + 1)
                V.tensor_tensor(w[:, 1, :], s, w[:, 0, :], ALU.subtract).then_inc(w_lo, 1)
            first_normalise(2, 0)
            first_variance(1, 1)
            var_eps(3)
            with dve.Fori(0, PAIRS - 2) as i:
                for r in range(2):
                    first(i, r, NB)
                piece_lo(i)
            for i in range(PAIRS - 2, PAIRS):
                for r in range(2):
                    first(i, r, NB - 2 * i - r)
                piece_lo(i)
            kq_lo(NB, 1, 0, kq_bank2[0])
            v_lo(NB, 1, 0, v_bank2[0])
            dve.wait_ge(w_lo, len(split) + PAIRS)
            V.memset(vs[1][:, :, C:C + 1], 1.0)
            dve.wait_ge(smalls_in, SMALLS)
            for u in range(UNITS):
                unit_max(0, u)
            row_max(0)
            for u in range(UNITS_EARLY - UNIT_OF[-1]):
                unit_max(1, u)
            for b in range(B):
                par, k0 = b % 2, b * NB
                projects, begin = b < B - 1, 1
                if b == 0:
                    attend(0, 2, (1 - par, 1), None)
                else:
                    attend(k0, 2, (1 - par, 1) if projects else None, NB - 1)
                    for nb in range(1, 1 + ROUTE_BLOCKS):
                        attend(k0 + nb, 2, (1 - par, nb + 1) if projects else None, nb - 1, (b - 1, nb - 1))
                    begin = 1 + ROUTE_BLOCKS
                with dve.Fori(begin, NB - 2) as nb:
                    attend(k0 + nb, 2, (1 - par, nb + 1) if projects else None, nb - 1)
                attend(k0 + NB - 2, 2 if b < B - 1 else 1, (1 - par, NB - 1) if projects else None, NB - 3)
                attend(k0 + NB - 1, 2 if b < B - 1 else 0, (par, 0) if b < B - 2 else None, NB - 2)

            def row_lo(f, ring):
                dve.wait_ge(thi_ready, f + 1)
                V.tensor_tensor(thl[:, 1, :, :], rowb[:, ring % 2, :, :], thl[:, 0, :, :], ALU.subtract
                                ).then_inc(tlo_ready, 1)

            def rows_t(f, ring):
                dve.wait_ge(ft_done, f + 2)
                V.tensor_copy(tt[:, ring % 2, :, :, :].rearrange("p h c n -> p (h c n)"), f16(x_bank)
                              ).then_inc(tt_ready, 1)

            def finish(f, ring, i):
                dve.wait_ge(w2_done, f * 4 + 6)
                V.tensor_tensor(yb[:, :, :], y_bank[ring % 2][:, :].rearrange("p (t c) -> p t c", t=FT), b2_s[:, :, :],
                                ALU.add).then_inc(y_read, 1)
                dve.wait_ge(y_read, f + 3)
                if ring >= 2:
                    dve.wait_ge(z_out[ring - 2], (i + 1) * (FT * 16))
                elif not isinstance(i, int) or i > 0:
                    dve.wait_ge(z_out[ring + 2], i * (FT * 16))
                for t in range(FT):
                    V.tensor_scalar(zb[ring % 2][:, t, :], yb[:, t, :], idw[:, ring, t, 0:1], None, ALU.mult
                                    ).then_inc(z_ready, 1)

            def mlp(f, ring, i, first, last, routes=False):
                if isinstance(f, int) and f == 1:
                    dve.wait_ge(res_ready, BLOCKS + 1)
                for p in range(HC // 2):
                    dve.wait_ge(hhi_ready, f * 4 + p + 1)
                    V.tensor_tensor(hlo[:, p % 2, :, :], h32[:, p % 2, :, :], hhi[:, p % 2, :, :], ALU.subtract
                                    ).then_inc(hlo_ready, 1)
                    if p == 0 and not last:
                        row_lo(f + 1, (ring + 1) % RING)
                    if p == 1 and not first:
                        finish(f - 1, (ring - 1) % RING, i if ring else i - 1)
                    if p == 2 and not last:
                        rows_t(f + 1, (ring + 1) % RING)
                    if first:
                        for part in ((0, 1), (2, 3), (4,), (5, 6))[p]:
                            end_block(BLOCKS - 1, NB - 1, part)
                    if routes and not first and (f - 1) * (HC // 2) + p in ROUTE_AT:
                        part, piece = ROUTE_AT[(f - 1) * (HC // 2) + p]
                        route(B - 1, part, (piece,))

            row_lo(0, 0)
            rows_t(0, 0)
            for i in range(ROUTED_BY):
                for ring in range(RING):
                    mlp(i * RING + ring, ring, i, i == ring == 0, False, True)
            with dve.Fori(ROUTED_BY, NI - 1) as i:
                for ring in range(RING):
                    mlp(i * RING + ring, ring, i, False, False)
            for ring in range(RING):
                mlp(NF - RING + ring, ring, NI - 1, False, ring == RING - 1)
            finish(NF - 1, RING - 1, NI - 1)

        @block.tensor
        def _(pe):
            mm = nc.tensor.matmul
            pe.wait_ge(consts, 6)
            pe.wait_ge(consts_dve, CONSTS_DVE)
            TERMS = ((0, 0), (0, 1), (1, 0))

            def y_transposes(to, y):
                for s in range(2):
                    for c in range(CC):
                        for t in range(QT):
                            at = (s * CC + c) * QB + t * P
                            last = nc.tensor.transpose(f16(to)[:, at:at + P], y[:, s, t, c * P:(c + 1) * P],
                                                       ident[:, :])
                last.then_inc(t_done, 1)

            def kq_products(to, y):
                for s, w in enumerate((wk_s, wq_s)):
                    for n, (a, c2) in enumerate(TERMS):
                        for c in range(CC):
                            last = mm(to[:, s * QB:(s + 1) * QB], w[:, a, c, :], y[:, c2, c, :],
                                      start=(n == 0 and c == 0), stop=(n == 2 and c == CC - 1))
                last.then_inc(kq_done, 1)

            def v_products(to, y):
                for t in range(QT):
                    for n, (a, c2) in enumerate(TERMS):
                        for c in range(CC):
                            last = mm(to[:, t * C:(t + 1) * C], y[:, a, c, t * P:(t + 1) * P], wv_s[:, c2, c, :],
                                      start=(n == 0 and c == 0), stop=(n == 2 and c == CC - 1))
                last.then_inc(v_done, 1)

            def first_transpose(h, r):
                pe.wait_ge(ylo_ready, h + 2)
                if not isinstance(h, int) or h > 1:
                    pe.wait_ge(yt_ready, h - 1)
                y_transposes(t_bank2[r], yhl2[r])

            def first_kq(h, r):
                pe.wait_ge(yt_ready, h + 1)
                if not isinstance(h, int) or h > 1:
                    pe.wait_ge(kqlo_ready, h - 1)
                kq_products(kq_bank2[r], yt2[r])

            def first_v(h, r):
                if not isinstance(h, int) or h > 0:
                    pe.wait_ge(vlo_ready, h)
                v_products(v_bank2[r], yt2[r])

            def transpose_y(h):
                pe.wait_ge(ylo_ready, h + 2)
                pe.wait_ge(vlo_ready, h + 1)
                y_transposes(p_bank, yhl)

            def project_kq(h):
                pe.wait_ge(yt_ready, h + 1)
                kq_products(p_bank, yt)

            def project_v(h):
                pe.wait_ge(kqlo_ready, h + 1)
                v_products(p_bank, yt)

            def scores(t, par, nb, j):
                pe.wait_ge(exp_done, t + 1)
                cols = bass.ds(nb * QB, QB)
                for m in range(2):
                    keys = slice((2 * j + m) * P, (2 * j + m + 1) * P)
                    o = s_bank[j % 2][:, m * QB:(m + 1) * QB]
                    mm(o, ka[par][:, keys], qa[par][:, cols], start=True, stop=False)
                    last = mm(o, kb[par][0:D + 1, keys], qb[par][0:D + 1, cols], start=False, stop=True)
                last.then_inc(s_done, 1)

            def unit(k, par, nb, u):
                pe.wait_ge(m_read, k * UNITS + u + 1)
                mm(m_bank[u % 2][:, :], qa[par][:, bass.ds(nb * QB + (u // 8) * P, P)],
                   ka[par][:, (u % 8) * 512:(u % 8 + 1) * 512], start=True, stop=True).then_inc(m_done, 1)

            def max_row(k):
                pe.wait_ge(negm_ready, k + 1)
                for i in range(QT):
                    last = mm(row_bank[D:D + 1, i * P:(i + 1) * P], negm[:, i:i + 1], ident[:, :], start=True, stop=True)
                last.then_inc(row_done, 1)

            def p_v_tile(par, j, m, i):
                v_hi1 = vs[par][:, 2 * j + m, 0:C + 1]
                v_lo = vs[par][:, 2 * j + m, VLO:VLO + C]
                ph = phi[:, j % 4, m, i * P:(i + 1) * P]
                pl = plo[:, j % 4, m, i * P:(i + 1) * P]
                begin, end = j == 0 and m == 0, j == STEPS - 1 and m == 1
                mm(o_bank[i][:, 0:C + 1], ph, v_hi1, start=begin, stop=False, skip_group_check=True)
                mm(o_bank[i][:, 0:C], ph, v_lo, start=False, stop=False, skip_group_check=True)
                return mm(o_bank[i][:, 0:C + 1], pl, v_hi1, start=False, stop=end, skip_group_check=True)

            def p_v(t, par, j):
                pe.wait_ge(lo_done, t + 5)
                for m in range(2):
                    for i in range(QT):
                        last = p_v_tile(par, j, m, i)
                last.then_inc(pv_done, 1)

            def p_v_at_edge(k, t, par, j):
                pe.wait_ge(lo_done, t + 5)
                for i in range(QT):
                    if j == 0:
                        pe.wait_ge(o_read, k * QT + i + 1)
                    for m in range(2):
                        last = p_v_tile(par, j, m, i)
                    if j == STEPS - 1 and i < QT - 1:
                        last.then_inc(o_done, 1)
                last.then_inc(pv_done, 1)

            def route_sums(b, e):
                pe.wait_ge(cnt_ready, b * RC_N + e + 1)
                o = r_bank[:, 0:3 * NT]
                if e < 8:
                    last = mm(o[:, 0:15], ones16[:, :], cnt[:, :], start=True, stop=True)
                elif e == 8:
                    mm(o[:, 0:NT], ones16[:, :], gt16[:, :], start=True, stop=True)
                    mm(o[:, NT:2 * NT], ones16[:, :], eq16[:, :], start=True, stop=True)
                    last = mm(o[:, 2 * NT:3 * NT], tri16[:, :], eq16[:, :], start=True, stop=True)
                else:
                    mm(o[:, 0:NT], ones16[:, :], sel16[:, :], start=True, stop=True)
                    last = mm(o[:, NT:2 * NT], tri16[:, :], sel16[:, :], start=True, stop=True)
                last.then_inc(tot_ready, 1)

            def attend(k, par, nb, following, second, projects, routed=None):
                u = UNITS_EARLY
                for j in range(STEPS):
                    t = k * STEPS + j
                    if j + 2 < STEPS:
                        scores(t + 2, par, nb, j + 2)
                    elif following:
                        if j == STEPS - 2:
                            pe.wait_ge(row_ready, k + 2)
                        scores(t + 2, *following, j + 2 - STEPS)
                    if j < STEPS - 2 and following:
                        for _ in range(UNIT_OF[j]):
                            unit(k + 1, *following, u)
                            u += 1
                        if j == STEPS - 3:
                            max_row(k + 1)
                    elif j >= STEPS - 2 and second:
                        for n in range(UNIT_OF[j]):
                            unit(k + 2, *second, sum(UNIT_OF[STEPS - 2:j]) + n)
                    if routed and routing_at(SUMS_AT, routed[1], j) is not None:
                        route_sums(routed[0], routing_at(SUMS_AT, routed[1], j))
                    if j in (0, STEPS - 1):
                        p_v_at_edge(k, t, par, j)
                    else:
                        p_v(t, par, j)
                    if projects:
                        if j == 7:
                            transpose_y(k + AHEAD)
                        elif j == 9:
                            project_kq(k + AHEAD)
                        elif j == 13:
                            project_v(k + AHEAD)

            def image_ready(b):
                pe.wait_ge(kqlo_ready, b * NB + NB)
                pe.wait_ge(vlo_ready, b * NB + NB + 1)

            def first(h, r, behind):
                first_v(h, r)
                first_kq(h + 1, 1 - r)
                if behind > 1:
                    first_transpose(h + 2, r)

            first_transpose(0, 0)
            first_transpose(1, 1)
            pe.wait_ge(w_lo, len(split))
            first_kq(0, 0)
            for h in range(2):
                first(h, h, NB)
            with pe.Fori(1, PAIRS - 1) as i:
                for r in range(2):
                    first(2 * i + r, r, NB)
            for r in range(2):
                first(NB - 2 + r, r, 2 - r)
            first_v(NB, 0)
            pe.wait_ge(smalls_in, SMALLS)
            pe.wait_ge(kqlo_ready, AHEAD)
            pe.wait_ge(vlo_ready, AHEAD + 1)
            for u in range(UNITS):
                unit(0, 0, 0, u)
            max_row(0)
            pe.wait_ge(row_ready, 1)
            for j in range(2):
                scores(j, 0, 0, j)
            for u in range(UNITS_EARLY):
                unit(1, 0, 1, u)
            for b in range(B):
                par, k0 = b % 2, b * NB
                projects, begin = b < B - 1, 0
                if b > 0:
                    attend(k0, par, 0, (par, 1), (par, 2), projects)
                    for nb in range(1, 1 + ROUTE_BLOCKS):
                        attend(k0 + nb, par, nb, (par, nb + 1), (par, nb + 2), projects, (b - 1, nb - 1))
                    begin = (1 + ROUTE_BLOCKS) // 2
                with pe.Fori(begin, PAIRS - 1) as i:
                    for r in range(2):
                        nb = 2 * i + r
                        attend(k0 + nb, par, nb, (par, nb + 1), (par, nb + 2), projects)
                after = [(1 - par, i) for i in range(2)] if projects else [None, None]
                attend(k0 + NB - 2, par, NB - 2, (par, NB - 1), after[0], projects)
                if projects:
                    image_ready(b + 1)
                attend(k0 + NB - 1, par, NB - 1, after[0], after[1], b < B - 2)

            def transpose_rows(f):
                pe.wait_ge(tlo_ready, f + 1)
                pe.wait_ge(tt_ready, f + 1)
                for h in range(2):
                    for c in range(CC):
                        for t in range(FT):
                            at = (h * CC + c) * FB + t * P
                            last = nc.tensor.transpose(f16(x_bank)[:, at:at + P], thl[:, h, t, c * P:(c + 1) * P],
                                                       ident[:, :])
                last.then_inc(ft_done, 1)

            def hidden(f, ring, p):
                if p == 0:
                    pe.wait_ge(tt_ready, f + 2)
                pe.wait_ge(gelu_done, f * 4 + p + 1)
                for hh in range(2):
                    units = slice((2 * p + hh) * P, (2 * p + hh + 1) * P)
                    for n, (a, c2) in enumerate(TERMS):
                        for c in range(CC):
                            last = mm(h_bank[p % 2][:, hh * FB:(hh + 1) * FB], w1_s[:, a, c, units],
                                      tt[:, ring % 2, c2, c, :], start=(n == 0 and c == 0),
                                      stop=(n == 2 and c == CC - 1))
                last.then_inc(h_done, 1)

            def second(f, ring, p):
                pe.wait_ge(hlo_ready, f * 4 + p + 3)
                if p == 0:
                    pe.wait_ge(y_read, f + 1)
                for hh in range(2):
                    for t in range(FT):
                        o = y_bank[ring % 2][:, t * C:(t + 1) * C]
                        for n, (a, c2) in enumerate(TERMS):
                            h = (hhi, hlo)[a][:, p % 2, hh, t * P:(t + 1) * P]
                            last = mm(o, h, w2_s[:, c2, 2 * p + hh, :], start=(p == hh == t == n == 0),
                                      stop=(p == 3 and hh == 1 and n == 2), skip_group_check=True)
                last.then_inc(w2_done, 1)

            def mlp(f, ring, last, routes=False):
                for p in range(HC // 2):
                    if p + 1 < HC // 2:
                        hidden(f, ring, p + 1)
                    elif not last:
                        hidden(f + 1, ring + 1, 0)
                    second(f, ring, p)
                    if p == 1 and not last:
                        transpose_rows(f + 1)
                    if routes and (f - 1) * (HC // 2) + p in SUMS_AT:
                        route_sums(B - 1, SUMS_AT[(f - 1) * (HC // 2) + p])

            transpose_rows(0)
            hidden(0, 0, 0)
            for i in range(ROUTED_BY):
                for ring in range(RING):
                    mlp(i * RING + ring, ring, False, True)
            with pe.Fori(ROUTED_BY, NI - 1) as i:
                for ring in range(RING):
                    mlp(i * RING + ring, ring, False)
            for ring in range(RING):
                mlp(NF - RING + ring, ring, ring == RING - 1)


def kernel(**inputs):
    import numpy as np
    import concourse.bacc as bacc
    from concourse.bass_utils import run_bass_kernel_spmd

    a = {k: np.asarray(v) for k, v in inputs.items()}
    wide = lambda v, n: np.ascontiguousarray(np.broadcast_to(v.reshape(1, -1), (P, n)))

    def by_rows(w):
        k, n = w.shape
        return np.ascontiguousarray(w.reshape(k // P, P, n).transpose(1, 0, 2).reshape(P, -1))

    def twice(v):
        return np.ascontiguousarray(np.concatenate([v, v], axis=-1))

    arrays = {
        "x": np.ascontiguousarray(a["x"].reshape(B, C, N).transpose(0, 2, 1).reshape(B * N, C)),
        "wq": by_rows(twice(a["L0_conv_wq"].T)),
        "wk": by_rows(twice(a["L0_conv_wk"].T)),
        "wv": by_rows(a["L0_conv_wv"].T),
        "bq": twice(a["L0_conv_bq"]).reshape(P, 1),
        "bk": twice(a["L0_conv_bk"]).reshape(P, 1),
        "bv": wide(a["L0_conv_bv"], C),
        "wr": wide(a["L0_ffn_wr"], C),
        "br": wide(a["L0_ffn_br"], 1),
        "w12": np.ascontiguousarray(np.concatenate([by_rows(a["L0_ffn_w1"]), by_rows(a["L0_ffn_w2"])], axis=1)),
        "b1": np.ascontiguousarray(a["L0_ffn_b1"].reshape(HC, P).T),
        "b2": wide(a["L0_ffn_b2"], C),
        "ones": np.ones((1, N), np.float16),
    }
    nc = bacc.Bacc("TRN2", target_bir_lowering=False, num_devices=1)
    args = {k: nc.dram_tensor(f"in_{k}", v.shape, F16 if k == "ones" else F32, kind="ExternalInput").ap()
            for k, v in arrays.items()}
    args["out"] = nc.dram_tensor("out_rows", (B * N, C), F32, kind="ExternalOutput").ap()
    build(nc, **args)
    r = run_bass_kernel_spmd(nc, [{f"in_{k}": v for k, v in arrays.items()}], core_ids=[0])
    rows = r.results[0]["out_rows"]
    return np.ascontiguousarray(rows.reshape(B, N, C).transpose(0, 2, 1)).reshape(B, C, 64, 64)
```
